# Optimizing a Trainium2 kernel written in Bass

```python
import numpy as np
import jax
import jax.numpy as jnp

def _softmax(x, axis=-1):
    return jax.nn.softmax(x, axis=axis)

def _gelu(x):
    return jax.nn.gelu(x, approximate=True)

def _silu(x):
    return jax.nn.silu(x)

def _sigmoid(x):
    return jax.nn.sigmoid(x)

def _layernorm(x, axis=-1, eps=1e-05):
    m = jnp.mean(x, axis=axis, keepdims=True)
    v = jnp.var(x, axis=axis, keepdims=True)
    return (x - m) / jnp.sqrt(v + eps)

def _scatter_add(tgt, idx, src, axis=0):
    return tgt.at[idx].add(src)

def _segment_sum(src, seg, n):
    return jax.ops.segment_sum(src, seg, n)
kernel_name = 'mk_gnn_preln_d1_gnn_r32_8fb63c'

def setup_inputs(seed: int=0):
    np.random.seed(seed)
    _w = jnp.asarray

    def _rec_inputs():
        import jax
        import jax.numpy as jnp
        _gk = jax.random.key(seed)
        x = -0.000202 + 1 * jax.random.normal(jax.random.fold_in(_gk, 1), (3125, 128), jnp.float32)
        src = jax.random.randint(jax.random.fold_in(_gk, 2), (100000,), 0, 3125, jnp.int32)
        dst = jax.random.randint(jax.random.fold_in(_gk, 3), (100000,), 0, 3125, jnp.int32)
        _o = jnp.argsort(dst, stable=True)
        src = src[_o]
        dst = dst[_o]
        edge_type_16 = jax.random.randint(jax.random.fold_in(_gk, 12), (100000,), 0, 16, jnp.int32)
        node_type_8 = jax.random.randint(jax.random.fold_in(_gk, 13), (3125,), 0, 8, jnp.int32)
        return (x, src, dst, edge_type_16, node_type_8)
    x, src, dst, edge_type_16, node_type_8 = _rec_inputs()

    def _L0_gnn_setup():
        import jax, jax.numpy as jnp
        import numpy as np
        N_NODES = 50000
        N_EDGES = 20000
        D = 128
        N_RELS = 16
        N_NTYPES = 8
        key = jax.random.key(seed)
        ks = jax.random.split(key, 9)
        return {'feats': jax.random.normal(ks[0], (N_NODES, D), dtype=jnp.float32), 'W_edge': jax.random.normal(ks[1], (N_RELS, D, D), dtype=jnp.float32) / np.sqrt(D), 'b_edge': jax.random.normal(ks[2], (N_RELS, D), dtype=jnp.float32) * 0.02, 'W_node': jax.random.normal(ks[3], (N_NTYPES, D, D), dtype=jnp.float32) / np.sqrt(D), 'b_node': jax.random.normal(ks[4], (N_NTYPES, D), dtype=jnp.float32) * 0.02, 'src': jax.random.randint(ks[5], (N_EDGES,), 0, N_NODES, dtype=jnp.int32), 'dst': jax.random.randint(ks[6], (N_EDGES,), 0, N_NODES, dtype=jnp.int32), 'ntypes': jax.random.randint(ks[7], (N_NODES,), 0, N_NTYPES, dtype=jnp.int32), 'etypes': jax.random.randint(ks[8], (N_EDGES,), 0, N_RELS, dtype=jnp.int32)}
    _L0_gnn_all = _L0_gnn_setup()
    _L0_gnn_in = {k: v for k, v in _L0_gnn_all.items() if k in ('W_edge', 'b_edge', 'W_node', 'b_node')}
    del _L0_gnn_all
    return {'x': x, 'src': src, 'dst': dst, 'edge_type_16': edge_type_16, 'node_type_8': node_type_8, 'L0_gnn_W_edge': _L0_gnn_in['W_edge'], 'L0_gnn_b_edge': _L0_gnn_in['b_edge'], 'L0_gnn_W_node': _L0_gnn_in['W_node'], 'L0_gnn_b_node': _L0_gnn_in['b_node']}

def reference(x, src, dst, edge_type_16, node_type_8, L0_gnn_W_edge, L0_gnn_b_edge, L0_gnn_W_node, L0_gnn_b_node):
    import jax
    import jax.numpy as jnp

    def _L0_gnn_ref(feats, W_edge, b_edge, W_node, b_node, src, dst, ntypes, etypes):
        import jax, jax.numpy as jnp
        import numpy as np
        N_NODES = 50000
        N_EDGES = 20000
        D = 128
        N_RELS = 16
        N_NTYPES = 8
        N, d = feats.shape
        T = W_edge.shape[0]
        hW = jnp.einsum('nd,tdf->tnf', feats, W_edge) + b_edge[:, None, :]
        msg = hW[etypes, src]
        seg = dst * T + etypes
        counts = jax.ops.segment_sum(jnp.ones(msg.shape[0], dtype=msg.dtype), seg, num_segments=N * T)
        msg = msg / counts[seg][:, None]
        agg = jax.ops.segment_sum(msg, dst, num_segments=N)
        hN = jnp.einsum('nd,tdf->tnf', feats, W_node) + b_node[:, None, :]
        out = hN[ntypes, jnp.arange(N)] + agg
        return jax.nn.relu(out)
    h = jnp.maximum(_layernorm(x, axis=-1), 0.0)
    x = x + _L0_gnn_ref(h, L0_gnn_W_edge, L0_gnn_b_edge, L0_gnn_W_node, L0_gnn_b_node, src, dst, node_type_8, edge_type_16)
    return x

_drawn_inputs = setup_inputs


def setup_inputs(seed=0):
    import zlib

    import numpy as np

    out = dict(_drawn_inputs(seed))
    spreads = {}
    factors = {'L0_gnn_b_node': 7.969}
    for name, (base, spread) in spreads.items():
        noise = np.random.default_rng([zlib.crc32(name.encode()), seed]).standard_normal(out[name].shape)
        drawn = base * np.exp(spread * noise) if base else spread * noise
        out[name] = jnp.asarray(drawn.astype(out[name].dtype))
    for name, factor in factors.items():
        out[name] = (out[name] * factor).astype(out[name].dtype)
    return out
```

```python
from contextlib import ExitStack

import concourse.bass as bass
from concourse import mybir
from concourse.alu_op_type import AluOpType as ALU

ACT = mybir.ActivationFunctionType
AX = mybir.AxisListType
F32 = mybir.dt.float32
BF16 = mybir.dt.bfloat16
I32 = mybir.dt.int32

P = 128
EPS = 1e-5
STEP = 32
SLOTS = 16
STAGE = 8
NSTAGE = STEP // STAGE
ONEHOTS = 4
RING_BLOCKS = 4
WIN_NODES = 8
GEN_NODES = 32
ds = bass.ds


def gnn_program(nc, x, src, dst, etype, ntype, w_edge, b_edge, w_node, b_node, out):
    N, D = x.shape
    E = src.shape[0]
    T = w_edge.shape[0]
    NTY = w_node.shape[0]
    assert D == P and WIN_NODES * T == P and E >= P
    NB = -(-N // P)
    NT = -(-E // P)
    assert -(-NT // STEP) == NB and NB >= 3
    PACE = P // STEP
    G = -(-NT // P)
    GF, GR = NT // P, NT % P
    FULL_ROWS = E // P - GF * P
    RL = GR or P
    OVERLAP = NT * P - E
    NROW = N - (NB - 1) * P
    BC = P * T
    RC = RING_BLOCKS * BC
    WIN = WIN_NODES * T
    GW = GEN_NODES * T
    GQ = BC // GW
    NCHUNK = 4
    EDGES = [NB * c // NCHUNK for c in range(NCHUNK + 1)]
    CH = [(EDGES[c], EDGES[c + 1]) for c in range(NCHUNK)]
    LAST = NB - 1

    table = nc.dram_tensor("h_table", (N, 3 * D), BF16, kind="Internal").ap()

    with ExitStack() as ctx:
        def sb(name, shape, dt):
            return ctx.enter_context(nc.sbuf_tensor(name, shape, dt))

        def pb(name, shape, dt=F32):
            return ctx.enter_context(nc.psum_tensor(name, shape, dt))

        def sem(name):
            return ctx.enter_context(nc.semaphore(name))

        x_sb = sb("x_sb", [P, NB, D], F32)
        h3 = sb("h3", [P, NB, 3, D], BF16)
        hT = sb("hT", [P, NB * P], F32)
        ring = sb("ring", [P, 2, RC + WIN], F32)
        flat = ring[:, :, :].rearrange("p a c -> p (a c)")
        at = [0]

        def scratch(n):
            at[0] += n
            assert at[0] <= 2 * (RC + WIN)
            return flat[:, at[0] - n:at[0]]

        h = scratch(NB * D).rearrange("p (b d) -> p b d", d=D)
        rem = scratch(NB * D).rearrange("p (b d) -> p b d", d=D)
        src_i = scratch(G * P).bitcast(I32).rearrange("p (g e) -> p g e", e=P)
        dst_i = scratch(G * P).bitcast(I32).rearrange("p (g e) -> p g e", e=P)
        ety_i = scratch(G * P).bitcast(I32).rearrange("p (g e) -> p g e", e=P)
        src_f = scratch(G * P).rearrange("p (g e) -> p g e", e=P)
        seg_f = scratch(G * P).rearrange("p (g e) -> p g e", e=P)
        rel_f = scratch(G * P).rearrange("p (g e) -> p g e", e=P)

        src_T = sb("src_T", [P, G * P], I32)
        rel_T = sb("rel_T", [P, G * P], F32)
        seg_T = sb("seg_T", [P, G * P], F32)
        off_row = sb("off_row", [1, G * P], I32)
        stage = sb("stage", [P, NSTAGE, STAGE], I32)
        rows = sb("rows", [P, SLOTS, 3, D], BF16)
        onehot = sb("onehot", [P, ONEHOTS, WIN], BF16)
        onehot_g = sb("onehot_g", [P, GW], BF16)
        iota_w = sb("iota_w", [P, WIN], BF16)
        iota_g = sb("iota_g", [P, GW], F32)
        win_neg = sb("win_neg", [P, 1], F32)
        ones = sb("ones", [P, P], BF16)
        one_f = sb("one_f", [P, 1], F32)
        zeros = sb("zeros", [P, BC], BF16)
        ident = sb("ident", [P, P], F32)
        part = sb("part", [P, 1], F32)
        eps = sb("eps", [P, 1], F32)
        pace = sb("pace", [P, G], F32)
        stats = sb("stats", [P, NB, 6], F32)
        mv = sb("mv", [P, NB, 2], F32)
        std = sb("std", [P, NB], F32)
        rstd = sb("rstd", [P, NB], F32)
        nbias = sb("nbias", [P, NB], F32)
        mn = sb("mn", [P, G], F32)
        mx = sb("mx", [P, G], F32)
        mn16 = sb("mn16", [P, G], F32)
        dev = sb("dev", [P, G], F32)
        bad = sb("bad", [P, 3, G], F32)
        badsum = sb("badsum", [P, 1], F32)
        flag = sb("flag", [1, 1], I32)
        off_i = sb("off_i", [P, G], I32)
        off_f = sb("off_f", [P, G], F32)
        w_e = sb("w_e", [P, T, D], F32)
        w_n = sb("w_n", [P, NTY, D], F32)
        b_e = sb("b_e", [T, D], F32)
        b_n = sb("b_n", [NTY, D], F32)
        nty = sb("nty", [P, NB], I32)
        nty_row = sb("nty_row", [NTY, NB * P], I32)
        nmask = sb("nmask", [P, NTY, NB], F32)
        sums = sb("sums", [P, T, P], F32)
        cnt_row = sb("cnt_row", [1, T, P], F32)
        hT_b = sb("hT_b", [P, P], F32)
        cnt1 = sb("cnt1", [P, T], F32)
        rcnt = sb("rcnt", [P, T], F32)
        has = sb("has", [P, T], F32)
        has_T = sb("has_T", [T, P], F32)
        nty_T = sb("nty_T", [NTY, P], F32)
        acc = sb("acc", [P, D], F32)
        outb = sb("outb", [P, D], F32)

        p_tile = [pb(f"p_tile{i}", [P, 512]) for i in range(4)]
        p_prod = [pb(f"p_prod{i}", [P, 512]) for i in range(2)]
        p_misc = pb("p_misc", [P, 512])
        p_aux = pb("p_aux", [P, 512])
        p_cnt = p_misc[:, 0:T]
        p_hasT = p_misc[0:T, 128:128 + P]
        p_bias = p_misc[:, 256:256 + D]

        s_xin = [sem(f"s_xin{c}") for c in range(NCHUNK)]
        s_xpad = sem("s_xpad")
        s_edges = sem("s_edges")
        s_w = sem("s_w")
        s_const = sem("s_const")
        s_var = sem("s_var")
        s_std = sem("s_std")
        s_norm = sem("s_norm")
        s_h = sem("s_h")
        s_hi = sem("s_hi")
        s_rem = sem("s_rem")
        s_mid = sem("s_mid")
        s_lo = sem("s_lo")
        s_table = sem("s_table")
        s_chain = sem("s_chain")
        s_achain = sem("s_achain")
        s_srcf = sem("s_srcf")
        s_segf = sem("s_segf")
        s_masked = sem("s_masked")
        s_relf = sem("s_relf")
        s_off = sem("s_off")
        s_pT = sem("s_pT")
        s_srcT = sem("s_srcT")
        s_relT = sem("s_relT")
        s_segT = sem("s_segT")
        s_offrow = sem("s_offrow")
        s_flag = sem("s_flag")
        s_htp = sem("s_htp")
        s_htc = sem("s_htc")
        s_zero = sem("s_zero")
        s_row = [sem(f"s_row{k}") for k in range(SLOTS)]
        s_staged = sem("s_staged")
        s_onehot = sem("s_onehot")
        s_tile = sem("s_tile")
        s_acc = sem("s_acc")
        s_prep = sem("s_prep")
        s_zeroed = sem("s_zeroed")
        s_cnt = sem("s_cnt")
        s_has = sem("s_has")
        s_hasT = sem("s_hasT")
        s_hasTc = sem("s_hasTc")
        s_prod = sem("s_prod")
        s_used = sem("s_used")
        s_dve = sem("s_dve")
        s_final = sem("s_final")
        s_out = sem("s_out")
        s_stored = sem("s_stored")
        s_gstaged = sem("s_gstaged")
        s_growd = sem("s_growd")
        s_goh = sem("s_goh")
        s_gmm = sem("s_gmm")
        s_gcopied = sem("s_gcopied")

        N_CONST = 8
        N_W = 7
        N_TAB = NCHUNK + 1
        HT_ROUNDS = -(-NB // 4)

        def tiles_of(s):
            return min(STEP, NT - s * STEP)

        def folds(s):
            return 0 if isinstance(s, int) and s < 1 else 2 * (s - 1)

        def acc_after(s):
            return (NT if isinstance(s, int) and s == LAST else STEP * s + STEP) + 2 * s

        def ring_col(b):
            return (b & (RING_BLOCKS - 1)) * BC

        block = ctx.enter_context(nc.Block())

        @block.sync
        def _(sp):
            for c, (a, b) in enumerate(CH):
                full = min(b, NB - 1)
                sp.dma_start(x_sb[:, a:full, :], x[a * P:full * P].rearrange("(b p) d -> p b d", p=P)).then_inc(s_xin[c], 16)
                if b == NB:
                    sp.wait_ge(s_xpad, 1)
                    sp.dma_start(x_sb[0:NROW, LAST, :], x[LAST * P:N]).then_inc(s_xin[c], 16)
            sp.dma_start(w_e[:], w_edge.rearrange("t d f -> d t f")).then_inc(s_w, 16)
            sp.dma_start(w_n[:], w_node.rearrange("t d f -> d t f")).then_inc(s_w, 16)
            sp.dma_start(b_e[:], b_edge).then_inc(s_w, 16)
            sp.dma_start(b_n[:], b_node).then_inc(s_w, 16)
            for c, (a, b) in enumerate(CH):
                sp.wait_ge(s_lo, c + 1)
                full = min(b, NB - 1)
                sp.dma_start(table[a * P:full * P].rearrange("(b p) w -> p b w", p=P),
                             h3[:, a:full].rearrange("p b k d -> p b (k d)")).then_inc(s_table, 16)
                if b == NB:
                    sp.dma_start(table[LAST * P:N], h3[0:NROW, LAST].rearrange("p k d -> p (k d)")).then_inc(s_table, 16)
            sp.sem_inc(s_stored, 1)

            def store(b, row, n):
                sp.wait_ge(s_final, b + 1)
                sp.dma_start(out[ds(row, n)], outb[0:n, :]).then_inc(s_out, 16)
                sp.wait_ge(s_out, (b + 1) * 16)
                sp.sem_inc(s_stored, 1)

            with sp.Fori(0, NB - 1) as b:
                store(b, b * P, P)
            store(LAST, LAST * P, NROW)

        @block.gpsimd
        def _(pool):
            nc.gpsimd.memset(eps[:], EPS).then_inc(s_const, 1)
            nc.gpsimd.memset(one_f[:], 1.0).then_inc(s_const, 1)
            nc.gpsimd.memset(ident[:], 1.0).then_inc(s_const, 1)
            pool.wait_ge(s_const, 3)
            nc.gpsimd.affine_select(out=ident[:], in_=ident[:], compare_op=ALU.is_equal, fill=0.0, base=0,
                                    pattern=[[-1, P]], channel_multiplier=1).then_inc(s_const, 1)
            nc.gpsimd.iota(pace[:], [[PACE * P, G]], base=0, channel_multiplier=PACE,
                           allow_small_or_imprecise_dtypes=True).then_inc(s_const, 1)
            nc.gpsimd.iota(part[:], [[0, 1]], base=0, channel_multiplier=1,
                           allow_small_or_imprecise_dtypes=True).then_inc(s_const, 1)
            nc.gpsimd.memset(ones[:], 1.0).then_inc(s_const, 1)
            nc.gpsimd.iota(iota_w[:], [[1, WIN]], base=0, channel_multiplier=0,
                           allow_small_or_imprecise_dtypes=True).then_inc(s_const, 1)
            if OVERLAP:
                pool.wait_ge(s_segf, 1)
                nc.gpsimd.affine_select(out=seg_f[0:RL, G - 1, 0:OVERLAP], in_=seg_f[0:RL, G - 1, 0:OVERLAP],
                                        compare_op=ALU.is_gt, fill=-1.0, base=NT - 1 - (G - 1) * P,
                                        pattern=[[0, OVERLAP]], channel_multiplier=-1).then_inc(s_masked, 1)
            nc.gpsimd.iota(iota_g[:], [[1, GW]], base=0, channel_multiplier=0,
                           allow_small_or_imprecise_dtypes=True)
            nc.gpsimd.memset(zeros[:], 0.0).then_inc(s_zero, 1)
            pool.wait_ge(s_table, 16 * N_TAB)
            pool.wait_ge(s_flag, 1)
            unordered = pool.value_load(flag[0:1, 0:1])

            def gather(slot, idx):
                pool.nop(nofuse=True)
                return nc.gpsimd.indirect_dma_start(rows[:, slot].rearrange("p k d -> p (k d)"), None, table,
                                                    bass.IndirectOffsetOnAxis(ap=idx, axis=0))

            def step(s, n):
                t0 = s * STEP
                for u in range(n):
                    if u % STAGE == 0:
                        pool.wait_ge(s_staged, s * NSTAGE + u // STAGE + 1)
                    if not (isinstance(s, int) and s == 0 and u < SLOTS):
                        pool.wait_ge(s_tile, t0 + u - SLOTS + 1)
                    gather(u % SLOTS, stage[:, u // STAGE, u % STAGE:u % STAGE + 1]).then_inc(s_row[u % SLOTS], 16)

            with pool.If(unordered < 1):
                step(0, STEP)
                with pool.Fori(1, LAST) as s:
                    step(s, STEP)
                step(LAST, tiles_of(LAST))
            with pool.Else():
                with pool.Fori(0, NB * GQ) as w:
                    with pool.Fori(0, NT) as t:
                        k = w * NT + t
                        pool.wait_ge(s_gstaged, k + 1)
                        gather(0, stage[:, 0, 0:1]).then_inc(s_growd, 16)

        @block.scalar
        def _(act):
            def mid(c):
                a, b = CH[c]
                act.wait_ge(s_rem, c + 1)
                nc.scalar.activation(h3[:, a:b, 1], rem[:, a:b], ACT.Copy).then_inc(s_mid, 1)

            act.dma_start(dst_i[:, 0:GF], dst[0:GF * P * P].rearrange("(g r e) -> r g e", r=P, e=P)).then_inc(s_edges, 16)
            act.dma_start(src_i[:, 0:GF], src[0:GF * P * P].rearrange("(g r e) -> r g e", r=P, e=P)).then_inc(s_edges, 16)
            act.dma_start(ety_i[:, 0:GF], etype[0:GF * P * P].rearrange("(g r e) -> r g e", r=P, e=P)).then_inc(s_edges, 16)
            for to, frm in ((dst_i, dst), (src_i, src), (ety_i, etype)):
                lo = GF * P * P
                if FULL_ROWS:
                    act.dma_start(to[0:FULL_ROWS, GF], frm[lo:lo + FULL_ROWS * P].rearrange("(r e) -> r e", e=P)).then_inc(s_edges, 16)
                if OVERLAP:
                    act.dma_start(to[RL - 1:RL, G - 1], frm[E - P:E].rearrange("(r e) -> r e", e=P)).then_inc(s_edges, 16)
            act.dma_start(nty[:, 0:NB - 1], ntype[0:(NB - 1) * P].rearrange("(b p) -> p b", p=P),
                          allow_slow_non_contiguous=True).then_inc(s_w, 16)
            act.wait_ge(s_xpad, 1)
            act.dma_start(nty[0:NROW, LAST:NB], ntype[LAST * P:N].rearrange("(p o) -> p o", o=1),
                          allow_slow_non_contiguous=True).then_inc(s_w, 16)
            act.dma_start(nty_row[:, 0:N], ntype.rearrange("(o n) -> o n", o=1).broadcast_to([NTY, N])).then_inc(s_w, 16)

            act.wait_ge(s_const, 1)
            for c, (a, b) in enumerate(CH):
                act.wait_ge(s_var, c + 1)
                nc.scalar.activation(std[:, a:b], mv[:, a:b, 1], ACT.Sqrt, bias=eps[:, 0:1]).then_inc(s_std, 1)
            for c, (a, b) in enumerate(CH):
                act.wait_ge(s_norm, c + 1)
                for i in range(a, b):
                    last = nc.scalar.activation(h[:, i], x_sb[:, i], ACT.Relu, bias=nbias[:, i:i + 1],
                                                scale=rstd[:, i:i + 1])
                last.then_inc(s_h, 1)
                act.wait_ge(s_h, c + 1)
                nc.scalar.activation(h3[:, a:b, 0], h[:, a:b], ACT.Copy).then_inc(s_hi, 1)
                if c:
                    mid(c - 1)
            mid(NCHUNK - 1)

            act.wait_ge(s_pT, 1)
            for k in range(-(-G // 4)):
                w = min(NT, 4 * (k + 1) * P) - 4 * k * P
                last = nc.scalar.activation(src_T[:, 4 * k * P:4 * k * P + w], p_tile[k][:, 0:w], ACT.Copy)
            last.then_inc(s_srcT, 1)

            def stage_copy(j, t):
                act.nop(nofuse=True)
                nc.scalar.activation(stage[:, j], src_T[:, ds(t, STAGE)], ACT.Copy).then_inc(s_staged, 1)

            act.wait_ge(s_srcT, 1)
            act.wait_ge(s_flag, 1)
            unordered = act.value_load(flag[0:1, 0:1])

            def prep(b, filled):
                filled()
                act.wait_ge(s_prod, b * 6 + 1)
                col = ring_col(b)
                act.nop(nofuse=True)
                nc.scalar.activation(sums[:], ring[:, 0, ds(col, BC)].rearrange("p (n t) -> p t n", t=T), ACT.Copy)
                nc.scalar.activation(cnt_row[:], ring[0:1, 1, ds(col, BC)].rearrange("p (n t) -> p t n", t=T), ACT.Copy)
                nc.scalar.activation(hT_b[:], hT[:, ds(b * P, P)], ACT.Copy).then_inc(s_prep, 1)
                act.wait_ge(s_prep, b + 1)
                act.nop(nofuse=True)
                nc.scalar.activation(ring[:, 0, ds(col, BC)], zeros[:], ACT.Copy)
                nc.scalar.activation(ring[:, 1, ds(col, BC)], zeros[:], ACT.Copy).then_inc(s_zeroed, 1)

            def hT_copies():
                for r in range(HT_ROUNDS):
                    act.wait_ge(s_htp, r + 1)
                    w = min(4, NB - 4 * r) * P
                    nc.scalar.activation(hT[:, 4 * r * P:4 * r * P + w], p_prod[r % 2][:, 0:w], ACT.Copy).then_inc(s_htc, 1)

            def stages_ahead(s, n):
                for j in range(n):
                    act.wait_ge(s_tile, s * STEP + (j + 1) * STAGE)
                    stage_copy(j, (s + 1) * STEP + j * STAGE)

            hT_copies()
            act.wait_ge(s_htc, HT_ROUNDS)
            with act.If(unordered < 1):
                for j in range(NSTAGE):
                    stage_copy(j, j * STAGE)
                stages_ahead(0, NSTAGE)
                with act.Fori(1, LAST - 1) as s:
                    stages_ahead(s, NSTAGE)
                    prep(s - 1, lambda: act.wait_ge(s_acc, acc_after(s)))
                stages_ahead(LAST - 1, -(-tiles_of(LAST) // STAGE))
                prep(LAST - 2, lambda: act.wait_ge(s_acc, acc_after(LAST - 1)))
                prep(LAST - 1, lambda: act.wait_ge(s_acc, acc_after(LAST)))
                prep(LAST, lambda: None)
            with act.Else():
                with act.Fori(0, NB) as b:
                    with act.Fori(0, GQ) as q:
                        w = b * GQ + q
                        with act.Fori(0, NT) as t:
                            act.wait_ge(s_gmm, w * (NT + 2) + t + 1)
                            act.nop(nofuse=True)
                            nc.scalar.activation(stage[:, 0, 0:1], src_T[:, ds(t, 1)], ACT.Copy).then_inc(s_gstaged, 1)
                    prep(b, lambda: act.wait_ge(s_gcopied, (b + 1) * GQ + 1))

        @block.vector
        def _(dve):
            links = [0]

            def link(ins):
                links[0] += 1
                ins.then_inc(s_chain, 1)
                dve.wait_ge(s_chain, links[0])

            nc.vector.memset(nty[:, LAST:NB], 0)
            if NT < G * P:
                nc.vector.memset(src_T[:, NT:G * P], 0)
            nc.vector.memset(nty_row[:, N:NB * P], 0)
            nc.vector.memset(x_sb[:, LAST], 0.0).then_inc(s_xpad, 1)

            def normalise(c):
                a, b = CH[c]
                dve.wait_ge(s_std, c + 1)
                link(nc.vector.reciprocal(rstd[:, a:b], std[:, a:b]))
                nc.vector.scalar_tensor_tensor(nbias[:, a:b], mv[:, a:b, 0], -1.0, rstd[:, a:b],
                                               ALU.mult, ALU.mult).then_inc(s_norm, 1)

            for c, (a, b) in enumerate(CH):
                dve.wait_ge(s_xin[c], 16 * (2 if b == NB else 1))
                for i in range(a, b):
                    last = nc.vector.bn_stats(stats[:, i], x_sb[:, i])
                link(last)
                for i in range(a, b):
                    last = nc.vector.bn_aggr(mv[:, i], stats[:, i])
                last.then_inc(s_var, 1)
                if c:
                    normalise(c - 1)
            normalise(NCHUNK - 1)

            parts = [(slice(0, P), slice(0, GF))] * bool(GF) + [(slice(0, GR), slice(GF, G))] * bool(GR)
            dve.wait_ge(s_edges, 16 * (3 + 3 * bool(FULL_ROWS) + 3 * bool(OVERLAP)))
            nc.vector.memset(bad[:], 0.0)
            for p, g in parts:
                nc.vector.tensor_copy(src_f[p, g], src_i[p, g])
                nc.vector.scalar_tensor_tensor(seg_f[p, g], dst_i[p, g], float(T), ety_i[p, g], ALU.mult, ALU.add)
                nc.vector.tensor_reduce(mn[p, g], dst_i[p, g], AX.X, ALU.min)
                last = nc.vector.tensor_reduce(mx[p, g], dst_i[p, g], AX.X, ALU.max)
            last.then_inc(s_segf, 1)
            dve.wait_ge(s_segf, 1)
            dve.wait_ge(s_const, N_CONST)
            for p, g in parts:
                nc.vector.tensor_scalar(mn16[p, g], mn[p, g], float(T), None, ALU.mult)
                nc.vector.tensor_copy(off_i[p, g], mn[p, g])
                last = nc.vector.tensor_tensor(dev[p, g], mn[p, g], pace[p, g], ALU.subtract)
            link(last)
            for p, g in parts:
                nc.vector.tensor_tensor(bad[p, 0, g], mx[p, g], mn[p, g], ALU.subtract)
                nc.vector.tensor_scalar(bad[p, 1, g], dev[p, g], float(-P), None, ALU.is_lt)
                nc.vector.tensor_scalar(bad[p, 2, g], dev[p, g], float(P - WIN_NODES), None, ALU.is_gt)
                last = nc.vector.tensor_scalar(off_i[p, g], off_i[p, g], RING_BLOCKS * P - 1, T.bit_length() - 1,
                                               ALU.bitwise_and, ALU.logical_shift_left)
            link(last)
            for p, g in parts:
                nc.vector.tensor_scalar(bad[p, 0, g], bad[p, 0, g], float(WIN_NODES - 1), None, ALU.is_gt)
                last = nc.vector.tensor_copy(off_f[p, g], off_i[p, g])
            link(last)
            nc.vector.tensor_reduce(badsum[:], bad[:].rearrange("p a g -> p (a g)"), AX.X, ALU.add).then_inc(s_off, 1)
            if OVERLAP:
                dve.wait_ge(s_masked, 1)
            for g in range(G):
                r = P if g < GF else GR
                last = nc.vector.tensor_scalar(rel_f[0:r, g], seg_f[0:r, g], mn16[0:r, g:g + 1], None, ALU.subtract)
            last.then_inc(s_relf, 1)

            def split(c):
                a, b = CH[c]
                dve.wait_ge(s_hi, c + 1)
                nc.vector.tensor_tensor(rem[:, a:b], h[:, a:b], h3[:, a:b, 0], ALU.subtract).then_inc(s_rem, 1)
                if c:
                    low(c - 1)

            def low(c):
                a, b = CH[c]
                dve.wait_ge(s_mid, c + 1)
                nc.vector.tensor_tensor(h3[:, a:b, 2], rem[:, a:b], h3[:, a:b, 1], ALU.subtract).then_inc(s_lo, 1)

            for c in range(NCHUNK):
                split(c)
            low(NCHUNK - 1)

            dve.wait_ge(s_pT, 4)
            for k in range(-(-G // 4)):
                w = (min(NT, 4 * (k + 1) * P) - 4 * k * P)
                nc.vector.tensor_copy(off_row[:, 4 * k * P:4 * k * P + w], (p_misc, p_aux)[k][0:1, 0:w])
            dve.wait_ge(s_pT, 5)
            nc.vector.tensor_copy(flag[:], p_tile[3][0:1, 511:512]).then_inc(s_flag, 1)
            dve.wait_ge(s_flag, 1)
            dve.wait_ge(s_relf, 1)
            for k in range(-(-G // 4)):
                w = min(NT, 4 * (k + 1) * P) - 4 * k * P
                last = nc.vector.tensor_copy(rel_T[:, 4 * k * P:4 * k * P + w], p_tile[2 + k][:, 0:w])
            link(last)
            for k in range(-(-G // 4)):
                w = min(NT, 4 * (k + 1) * P) - 4 * k * P
                last = nc.vector.tensor_copy(seg_T[:, 4 * k * P:4 * k * P + w], p_prod[k][:, 0:w])
            last.then_inc(s_segT, 1)
            dve.wait_ge(s_w, 16 * N_W)
            for t in range(NTY):
                nc.vector.tensor_scalar(nmask[:, t], nty[:], float(t), None, ALU.is_equal)
            dve.wait_ge(s_htp, HT_ROUNDS)
            link(nc.vector.memset(ring[:], 0.0))
            nc.vector.memset(win_neg[:], 0.0).then_inc(s_gcopied, 1)
            dve.wait_ge(s_gcopied, 1)
            dve.wait_ge(s_zero, 1)
            dve.sem_inc(s_used, 2)
            unordered = dve.value_load(flag[0:1, 0:1])

            def make_onehot(t, u, first):
                if not first:
                    dve.wait_ge(s_tile, t - ONEHOTS + 1)
                nc.vector.tensor_scalar(onehot[:, u % ONEHOTS], iota_w[:], rel_T[:, ds(t, 1)], None,
                                        ALU.is_equal).then_inc(s_onehot, 1)

            N_LINK = 1 + 1 + 1 + T + NTY

            def block_pieces(b):
                k = [0]

                def chain(ins):
                    k[0] += 1
                    ins.then_inc(s_dve, 1)
                    dve.wait_ge(s_dve, b * N_LINK + k[0])

                def counts():
                    dve.wait_ge(s_cnt, b + 1)
                    chain(nc.vector.tensor_scalar(cnt1[:], p_cnt, 1.0, None, ALU.max))
                    nc.vector.tensor_scalar(has[:], p_cnt, 1.0, None, ALU.min).then_inc(s_has, 1)
                    chain(nc.vector.reciprocal(rcnt[:], cnt1[:]))

                def flags():
                    dve.wait_ge(s_hasT, b + 1)
                    nc.vector.tensor_copy(has_T[:], p_hasT)
                    nc.vector.tensor_scalar(nty_T[:], nty_row[:, ds(b * P, P)], part[0:NTY, 0:1], None,
                                            ALU.is_equal).then_inc(s_hasTc, 1)

                def group(g):
                    dve.wait_ge(s_prod, b * 6 + g + 2)
                    if g == 0:
                        chain(nc.vector.tensor_copy(acc[:], p_bias))
                    for j in range(4):
                        w = (rcnt[:, 4 * g + j:4 * g + j + 1] if g < 4 else
                             nmask[:, 4 * (g - 4) + j, ds(b, 1)])
                        ins = nc.vector.scalar_tensor_tensor(acc[:], p_prod[g % 2][:, j * D:(j + 1) * D], w, acc[:],
                                                             ALU.mult, ALU.add)
                        chain(ins)
                    dve.sem_inc(s_used, 1)

                def final():
                    assert k[0] == N_LINK
                    dve.wait_ge(s_stored, b + 1)
                    nc.vector.scalar_tensor_tensor(outb[:], acc[:], 0.0, x_sb[:, ds(b, 1)].rearrange("p o d -> p (o d)"), ALU.max, ALU.add).then_inc(s_final, 1)

                def last_group():
                    group(5)
                    final()

                return {4: counts, 8: flags, 11: lambda: group(0), 14: lambda: group(1), 17: lambda: group(2),
                        20: lambda: group(3), 23: lambda: group(4), 26: last_group}

            off_reg = [dve.alloc_register(f"off{u}") for u in range(STAGE)]

            def step(s, n, pieces, fold):
                t0 = s * STEP
                left = dict(pieces)
                for u in range(n):
                    if u % STAGE == 0:
                        m = min(STAGE, n - u)
                        dve.reg_load(off_reg[0:m], off_row[0:1, ds(t0 + u, m)])
                        off = [dve.snap(r, min_val=0, max_val=RC - T) for r in off_reg[0:m]]
                    if not (isinstance(s, int) and t0 + u + 2 >= NT):
                        make_onehot(t0 + u + 2, u + 2, isinstance(s, int) and t0 + u + 2 < ONEHOTS)
                    dve.wait_ge(s_tile, t0 + u + 1)
                    if not (isinstance(s, int) and s == 0 and u == 0):
                        dve.wait_ge(s_acc, t0 + u + folds(s))
                    w = ring[:, :, ds(off[u % STAGE], WIN)]
                    nc.vector.tensor_tensor(w, w, p_tile[u % 4][:, 0:2 * WIN].rearrange("p (a c) -> p a c", a=2),
                                            ALU.add).then_inc(s_acc, 1)
                    if u in left:
                        left.pop(u)()
                for f in left.values():
                    f()
                if fold:
                    if not (isinstance(s, int) and s == 1):
                        dve.wait_ge(s_zeroed, s - 1)
                    done = acc_after(s) - 2
                    dve.wait_ge(s_acc, done)
                    nc.vector.tensor_tensor(ring[:, :, 0:WIN], ring[:, :, 0:WIN], ring[:, :, RC:RC + WIN],
                                            ALU.add).then_inc(s_acc, 1)
                    dve.wait_ge(s_acc, done + 1)
                    nc.vector.memset(ring[:, :, RC:RC + WIN], 0.0).then_inc(s_acc, 1)

            with dve.If(unordered < 1):
                make_onehot(0, 0, True)
                make_onehot(1, 1, True)
                step(0, STEP, {}, False)
                step(1, STEP, {}, True)
                if LAST > 2:
                    with dve.Fori(2, LAST) as s:
                        step(s, STEP, block_pieces(s - 2), True)
                step(LAST, tiles_of(LAST), block_pieces(LAST - 2), True)
                for b in (LAST - 1, LAST):
                    for f in block_pieces(b).values():
                        f()
            with dve.Else():
                with dve.Fori(0, NB) as b:
                    with dve.Fori(0, GQ) as q:
                        w = b * GQ + q
                        with dve.Fori(0, NT) as t:
                            dve.wait_ge(s_gmm, w * (NT + 2) + t + 1)
                            nc.vector.tensor_scalar(onehot_g[:], iota_g[:], seg_T[:, ds(t, 1)], win_neg[:, 0:1],
                                                    ALU.subtract, ALU.is_equal).then_inc(s_goh, 1)
                        dve.wait_ge(s_gmm, (w + 1) * (NT + 2))
                        for a in range(2):
                            nc.vector.tensor_copy(ring[:, a, ds(ring_col(b) + q * GW, GW)], p_tile[a][:])
                        nc.vector.tensor_scalar(win_neg[:], win_neg[:], float(-GW), None, ALU.add).then_inc(s_gcopied, 1)
                        dve.wait_ge(s_gcopied, w + 2)
                    for f in block_pieces(b).values():
                        f()

        @block.tensor
        def _(pe):
            def turn(src3, banks):
                for g in range(G):
                    r = P if g < GF else GR
                    last = nc.tensor.transpose(banks[g // 4][:, (g % 4) * P:(g % 4) * P + r], src3[0:r, g], ident[0:r, 0:r])
                return last

            pe.wait_ge(s_const, N_CONST)
            pe.wait_ge(s_segf, 1)
            turn(src_f, p_tile[0:2]).then_inc(s_pT, 1)
            if OVERLAP:
                pe.wait_ge(s_masked, 1)
            pe.wait_ge(s_relf, 1)
            turn(rel_f, p_tile[2:4]).then_inc(s_pT, 1)
            turn(seg_f, p_prod).then_inc(s_pT, 1)
            for g in range(G):
                r = P if g < GF else GR
                last = nc.tensor.matmul((p_misc, p_aux)[g // 4][0:1, (g % 4) * P:(g % 4) * P + r],
                                        lhsT=off_f[0:r, g:g + 1], rhs=ident[0:r, 0:r], start=True, stop=True)
            last.then_inc(s_pT, 1)
            nc.tensor.matmul(p_tile[3][0:1, 511:512], lhsT=badsum[:], rhs=one_f[:], start=True, stop=True).then_inc(s_pT, 1)
            pe.wait_ge(s_h, NCHUNK)
            pe.wait_ge(s_segT, 1)
            for r in range(HT_ROUNDS):
                if r >= 2:
                    pe.wait_ge(s_htc, r - 1)
                for i in range(4 * r, min(4 * r + 4, NB)):
                    last = nc.tensor.transpose(p_prod[r % 2][:, (i % 4) * P:(i % 4 + 1) * P], h[:, i], ident[:])
                last.then_inc(s_htp, 1)
            pe.wait_ge(s_htc, HT_ROUNDS)
            pe.wait_ge(s_srcT, 1)
            pe.wait_ge(s_w, 16 * N_W)
            pe.sem_inc(s_prod, 1)
            pe.wait_ge(s_flag, 1)
            unordered = pe.value_load(flag[0:1, 0:1])

            def sums_of(bank_s, bank_c, slot, hot, start, last):
                for k in range(3):
                    nc.tensor.matmul(bank_s, lhsT=rows[:, slot, k], rhs=hot, start=start and k == 0, stop=last and k == 2)
                return nc.tensor.matmul(bank_c, lhsT=ones[:], rhs=hot, start=start, stop=last)

            def block_pieces(b):
                def counts():
                    pe.wait_ge(s_prep, b + 1)
                    pe.wait_ge(s_used, b * 6 + 2)
                    for t in range(T):
                        last = nc.tensor.matmul(p_cnt[:, t:t + 1], lhsT=cnt_row[:, t], rhs=one_f[0:1, :], start=True, stop=True)
                    last.then_inc(s_cnt, 1)

                def flags():
                    pe.wait_ge(s_has, b + 1)
                    nc.tensor.transpose(p_hasT, has[:], ident[:]).then_inc(s_hasT, 1)

                def bias():
                    pe.wait_ge(s_hasTc, b + 1)
                    nc.tensor.matmul(p_bias, lhsT=has_T[:], rhs=b_e[:], start=True, stop=False)
                    nc.tensor.matmul(p_bias, lhsT=nty_T[:], rhs=b_n[:], start=False, stop=True)

                def group(g):
                    pe.wait_ge(s_used, b * 6 + g + 1)
                    if g < 4:
                        for j in range(4):
                            last = nc.tensor.matmul(p_prod[g % 2][:, j * D:(j + 1) * D], lhsT=sums[:, 4 * g + j],
                                                    rhs=w_e[:, 4 * g + j], start=True, stop=True)
                    else:
                        j = 4 * (g - 4)
                        last = nc.tensor.matmul(p_prod[g % 2][:], lhsT=hT_b[:],
                                                rhs=w_n[:, j:j + 4].rearrange("p t f -> p (t f)"), start=True, stop=True)
                    last.then_inc(s_prod, 1)

                def first_group():
                    bias()
                    group(0)

                return {2: counts, 6: flags, 9: first_group, 12: lambda: group(1), 15: lambda: group(2),
                        18: lambda: group(3), 21: lambda: group(4), 24: lambda: group(5)}

            def step(s, n, pieces):
                t0 = s * STEP
                left = dict(pieces)
                for u in range(n):
                    pe.wait_ge(s_row[u % SLOTS], (s * (STEP // SLOTS) + u // SLOTS + 1) * 16)
                    pe.wait_ge(s_onehot, t0 + u + 1)
                    if not (isinstance(s, int) and s == 0 and u < 4):
                        pe.wait_ge(s_acc, t0 + u - 3 + folds(s if u >= 4 else s - 1))
                    sums_of(p_tile[u % 4][:, 0:WIN], p_tile[u % 4][:, WIN:2 * WIN], u % SLOTS,
                            onehot[:, u % ONEHOTS], True, True).then_inc(s_tile, 1)
                    if u in left:
                        left.pop(u)()
                for f in left.values():
                    f()

            with pe.If(unordered < 1):
                step(0, STEP, {})
                step(1, STEP, {})
                if LAST > 2:
                    with pe.Fori(2, LAST) as s:
                        step(s, STEP, block_pieces(s - 2))
                step(LAST, tiles_of(LAST), block_pieces(LAST - 2))
                for b in (LAST - 1, LAST):
                    for f in block_pieces(b).values():
                        f()
            with pe.Else():
                with pe.Fori(0, NB) as b:
                    with pe.Fori(0, GQ) as q:
                        w = b * GQ + q
                        pe.wait_ge(s_gcopied, w + 1)
                        nc.tensor.matmul(p_tile[0][:], lhsT=zeros[:, 0:P], rhs=zeros[:, 0:GW], start=True, stop=False)
                        nc.tensor.matmul(p_tile[1][:], lhsT=zeros[:, 0:P], rhs=zeros[:, 0:GW], start=True, stop=False).then_inc(s_gmm, 1)
                        with pe.Fori(0, NT) as t:
                            k = w * NT + t
                            pe.wait_ge(s_growd, (k + 1) * 16)
                            pe.wait_ge(s_goh, k + 1)
                            sums_of(p_tile[0][:], p_tile[1][:], 0, onehot_g[:], False, False).then_inc(s_gmm, 1)
                        nc.tensor.matmul(p_tile[0][:], lhsT=zeros[:, 0:P], rhs=zeros[:, 0:GW], start=False, stop=True)
                        nc.tensor.matmul(p_tile[1][:], lhsT=zeros[:, 0:P], rhs=zeros[:, 0:GW], start=False, stop=True).then_inc(s_gmm, 1)
                    for f in block_pieces(b).values():
                        f()


_INS = ["x", "src", "dst", "edge_type_16", "node_type_8", "L0_gnn_W_edge", "L0_gnn_b_edge", "L0_gnn_W_node", "L0_gnn_b_node"]


def kernel(**inputs):
    import numpy as np
    import concourse.bacc as bacc
    from concourse.bass_utils import run_bass_kernel_spmd

    nc = bacc.Bacc("TRN2", target_bir_lowering=False, num_devices=1)
    arrays, args = {}, []
    for name in _INS:
        a = np.ascontiguousarray(inputs[name])
        arrays[f"in_{name}"] = a
        args.append(nc.dram_tensor(f"in_{name}", a.shape, mybir.dt.from_np(a.dtype), kind="ExternalInput").ap())
    out = nc.dram_tensor("out_0", inputs["x"].shape, F32, kind="ExternalOutput").ap()
    gnn_program(nc, *args, out)
    r = run_bass_kernel_spmd(nc, [arrays], core_ids=[0])
    return r.results[0]["out_0"]
```

```python
from contextlib import ExitStack

import concourse.bass as bass
from concourse import mybir
from concourse.alu_op_type import AluOpType as ALU

ACT = mybir.ActivationFunctionType
AX = mybir.AxisListType
F32 = mybir.dt.float32
BF16 = mybir.dt.bfloat16
I32 = mybir.dt.int32

P = 128
EPS = 1e-5
STEP = 32
SLOTS = 16
FREED = 4
STAGE = 8
NSTAGE = STEP // STAGE
ONEHOTS = 16
AHEAD = 8
SLACK = 8
RING_BLOCKS = 4
WIN_NODES = 8
GEN_NODES = 32
ds = bass.ds


def gnn_program(nc, x, src, dst, etype, ntype, w_edge, b_edge, w_node, b_node, out):
    N, D = x.shape
    E = src.shape[0]
    T = w_edge.shape[0]
    NTY = w_node.shape[0]
    assert D == P and WIN_NODES * T == P and E >= P
    NB = -(-N // P)
    NT = -(-E // P)
    assert -(-NT // STEP) == NB and NB >= 5 and NT - (NB - 1) * STEP >= SLACK
    PACE = P // STEP
    G = -(-NT // P)
    GF, GR = NT // P, NT % P
    FULL_ROWS = E // P - GF * P
    RL = GR or P
    OVERLAP = NT * P - E
    NROW = N - (NB - 1) * P
    BC = P * T
    RC = RING_BLOCKS * BC
    WIN = WIN_NODES * T
    GW = GEN_NODES * T
    GQ = BC // GW
    NCHUNK = 4
    EDGES = [NB * c // NCHUNK for c in range(NCHUNK + 1)]
    CH = [(EDGES[c], EDGES[c + 1]) for c in range(NCHUNK)]
    LAST = NB - 1

    table = nc.dram_tensor("h_table", (N, 3 * D), BF16, kind="Internal").ap()

    with ExitStack() as ctx:
        def sb(name, shape, dt):
            return ctx.enter_context(nc.sbuf_tensor(name, shape, dt))

        def pb(name, shape, dt=F32):
            return ctx.enter_context(nc.psum_tensor(name, shape, dt))

        def sem(name):
            return ctx.enter_context(nc.semaphore(name))

        x_sb = sb("x_sb", [P, NB, D], F32)
        h3 = sb("h3", [P, NB, 3, D], BF16)
        hT = sb("hT", [P, NB * P], F32)
        ring = sb("ring", [P, 2, RC + WIN], F32)
        sums = sb("sums", [P, T, P], F32)
        cnt_row = sb("cnt_row", [P, T, P], F32)

        def scratch(space, start, dt, *shape):
            n = shape[0] * shape[1]
            v = space[:, start:start + n]
            v = v.bitcast(I32) if dt is I32 else v
            return v.rearrange("p (a b) -> p a b", b=shape[1])

        late = RC // 2
        late_s, late_c = ring[:, 0, late:], ring[:, 1, late:]
        sums_v = sums[:].rearrange("p t n -> p (t n)")
        cnt_v = cnt_row[:].rearrange("p t n -> p (t n)")
        GE = G * P
        assert NB * D + GE <= late + WIN and 2 * GE <= BC
        h = scratch(late_s, 0, F32, NB, D)
        rem = scratch(late_c, 0, F32, NB, D)
        seg_f = scratch(late_s, NB * D, F32, G, P)
        rel_f = scratch(late_c, NB * D, F32, G, P)
        src_i = scratch(sums_v, 0, I32, G, P)
        dst_i = scratch(sums_v, GE, I32, G, P)
        ety_i = scratch(cnt_v, 0, I32, G, P)
        src_f = scratch(cnt_v, GE, F32, G, P)

        src_T = sb("src_T", [P, G * P], I32)
        rel_T = sb("rel_T", [P, G * P], F32)
        seg_T = sb("seg_T", [P, G * P], F32)
        off_row = sb("off_row", [1, G * P], I32)
        stage = sb("stage", [P, NSTAGE, STAGE], I32)
        rows = sb("rows", [P, SLOTS, 3, D], BF16)
        onehot = sb("onehot", [P, ONEHOTS, WIN], BF16)
        onehot_g = sb("onehot_g", [P, GW], BF16)
        iota_w = sb("iota_w", [P, WIN], BF16)
        iota_g = sb("iota_g", [P, GW], F32)
        win_neg = sb("win_neg", [P, 1], F32)
        ones = sb("ones", [P, P], BF16)
        one_f = sb("one_f", [P, 1], F32)
        zeros = sb("zeros", [P, BC], BF16)
        ident = sb("ident", [P, P], F32)
        part = sb("part", [P, 1], F32)
        eps = sb("eps", [P, 1], F32)
        pace = sb("pace", [P, G], F32)
        stats = sb("stats", [P, NB, 6], F32)
        mv = sb("mv", [P, NB, 2], F32)
        std = sb("std", [P, NB], F32)
        rstd = sb("rstd", [P, NB], F32)
        nbias = sb("nbias", [P, NB], F32)
        mn = sb("mn", [P, G], F32)
        mx = sb("mx", [P, G], F32)
        mn16 = sb("mn16", [P, G], F32)
        dev = sb("dev", [P, G], F32)
        bad = sb("bad", [P, 3, G], F32)
        badsum = sb("badsum", [P, 1], F32)
        flag = sb("flag", [1, 1], I32)
        off_i = sb("off_i", [P, G], I32)
        off_f = sb("off_f", [P, G], F32)
        w_e = sb("w_e", [P, T, D], F32)
        w_n = sb("w_n", [P, NTY, D], F32)
        b_e = sb("b_e", [T, D], F32)
        b_n = sb("b_n", [NTY, D], F32)
        nty = sb("nty", [P, NB], I32)
        nty_row = sb("nty_row", [NTY, NB * P], I32)
        nmask = sb("nmask", [P, NTY, NB], F32)
        hT_b = sb("hT_b", [P, P], F32)
        cnt1 = sb("cnt1", [P, T], F32)
        rcnt = sb("rcnt", [P, T], F32)
        has = sb("has", [P, T], F32)
        has_T = sb("has_T", [T, P], F32)
        nty_T = sb("nty_T", [NTY, P], F32)
        acc = sb("acc", [P, 2, D], F32)
        outb = sb("outb", [P, D], F32)

        p_tile = [pb(f"p_tile{i}", [P, 512]) for i in range(4)]
        p_prod = [pb(f"p_prod{i}", [P, 512]) for i in range(2)]
        p_misc = pb("p_misc", [P, 512])
        p_aux = pb("p_aux", [P, 512])
        p_cnt = p_misc[:, 0:T]
        p_hasT = p_misc[0:T, 128:128 + P]
        p_bias = p_misc[:, 256:256 + D]

        s_xin = [sem(f"s_xin{c}") for c in range(NCHUNK)]
        s_xpad = sem("s_xpad")
        s_edges = sem("s_edges")
        s_w = sem("s_w")
        s_const = sem("s_const")
        s_var = sem("s_var")
        s_std = sem("s_std")
        s_h = sem("s_h")
        s_hi = sem("s_hi")
        s_rem = sem("s_rem")
        s_mid = sem("s_mid")
        s_lo = sem("s_lo")
        s_y = sem("s_y")
        s_conv = sem("s_conv")
        s_ring0 = sem("s_ring0")
        s_ring1 = sem("s_ring1")
        s_table = sem("s_table")
        s_chain = sem("s_chain")
        s_relf = sem("s_relf")
        s_off = sem("s_off")
        s_pT = sem("s_pT")
        s_srcT = sem("s_srcT")
        s_relT = sem("s_relT")
        s_segT = sem("s_segT")
        s_offrow = sem("s_offrow")
        s_flag = sem("s_flag")
        s_htp = sem("s_htp")
        s_htc = sem("s_htc")
        s_zero = sem("s_zero")
        s_row = [sem(f"s_row{k}") for k in range(SLOTS)]
        s_staged = sem("s_staged")
        s_onehot = sem("s_onehot")
        s_tile = sem("s_tile")
        s_acc = sem("s_acc")
        s_prep = sem("s_prep")
        s_zeroed = sem("s_zeroed")
        s_cnt = sem("s_cnt")
        s_has = sem("s_has")
        s_hasT = sem("s_hasT")
        s_hasTc = sem("s_hasTc")
        s_prod = sem("s_prod")
        s_used = sem("s_used")
        s_rc = sem("s_rc")
        s_dve = sem("s_dve")
        s_sum = sem("s_sum")
        s_final = sem("s_final")
        s_out = sem("s_out")
        s_stored = sem("s_stored")
        s_gstaged = sem("s_gstaged")
        s_growd = sem("s_growd")
        s_goh = sem("s_goh")
        s_gmm = sem("s_gmm")
        s_gcopied = sem("s_gcopied")

        N_CONST = 8
        N_EDGE_DMAS = 3 * (1 + bool(FULL_ROWS) + bool(OVERLAP))
        N_CONV = 2 + bool(OVERLAP)
        parts = [(slice(0, P), slice(0, GF)), (slice(0, GR), slice(GF, G))][:1 + bool(GR)]
        N_W = 7
        N_TAB = NCHUNK + 1
        HT_ROUNDS = -(-NB // 4)

        def tiles_of(s):
            return min(STEP, NT - s * STEP)

        def folds(s, u):
            if u >= SLACK:
                return 2 * s
            return 0 if isinstance(s, int) and s == 0 else 2 * (s - 1)

        def block_in_ring(s):
            return s * STEP + SLACK + 2 * s

        def ring_col(b):
            return (b & (RING_BLOCKS - 1)) * BC

        block = ctx.enter_context(nc.Block())

        @block.sync
        def _(sp):
            for c, (a, b) in enumerate(CH):
                full = min(b, NB - 1)
                sp.dma_start(x_sb[:, a:full, :], x[a * P:full * P].rearrange("(b p) d -> p b d", p=P)).then_inc(s_xin[c], 16)
                if b == NB:
                    sp.wait_ge(s_xpad, 1)
                    sp.dma_start(x_sb[0:NROW, LAST, :], x[LAST * P:N]).then_inc(s_xin[c], 16)
            sp.dma_start(w_e[:], w_edge.rearrange("t d f -> d t f")).then_inc(s_w, 16)
            sp.dma_start(w_n[:], w_node.rearrange("t d f -> d t f")).then_inc(s_w, 16)
            sp.dma_start(b_e[:], b_edge).then_inc(s_w, 16)
            sp.dma_start(b_n[:], b_node).then_inc(s_w, 16)
            for c, (a, b) in enumerate(CH):
                sp.wait_ge(s_lo, c + 1)
                full = min(b, NB - 1)
                sp.dma_start(table[a * P:full * P].rearrange("(b p) w -> p b w", p=P),
                             h3[:, a:full].rearrange("p b k d -> p b (k d)")).then_inc(s_table, 16)
                if b == NB:
                    sp.dma_start(table[LAST * P:N], h3[0:NROW, LAST].rearrange("p k d -> p (k d)")).then_inc(s_table, 16)
            sp.sem_inc(s_stored, 1)

            def store(b, row, n):
                sp.wait_ge(s_final, b + 1)
                sp.dma_start(out[ds(row, n)], outb[0:n, :]).then_inc(s_out, 16)
                sp.wait_ge(s_out, (b + 1) * 16)
                sp.sem_inc(s_stored, 1)

            with sp.Fori(0, NB - 1) as b:
                store(b, b * P, P)
            store(LAST, LAST * P, NROW)

        @block.gpsimd
        def _(pool):
            nc.gpsimd.memset(eps[:], EPS).then_inc(s_const, 1)
            nc.gpsimd.memset(one_f[:], 1.0).then_inc(s_const, 1)
            nc.gpsimd.memset(ident[:], 1.0).then_inc(s_const, 1)
            pool.wait_ge(s_const, 3)
            nc.gpsimd.affine_select(out=ident[:], in_=ident[:], compare_op=ALU.is_equal, fill=0.0, base=0,
                                    pattern=[[-1, P]], channel_multiplier=1).then_inc(s_const, 1)
            nc.gpsimd.iota(pace[:], [[PACE * P, G]], base=0, channel_multiplier=PACE,
                           allow_small_or_imprecise_dtypes=True).then_inc(s_const, 1)
            nc.gpsimd.iota(part[:], [[0, 1]], base=0, channel_multiplier=1,
                           allow_small_or_imprecise_dtypes=True).then_inc(s_const, 1)
            nc.gpsimd.memset(ones[:], 1.0).then_inc(s_const, 1)
            nc.gpsimd.iota(iota_w[:], [[1, WIN]], base=0, channel_multiplier=0,
                           allow_small_or_imprecise_dtypes=True).then_inc(s_const, 1)
            nc.gpsimd.memset(ring[:, :, 0:late], 0.0).then_inc(s_ring0, 1)
            pool.wait_ge(s_edges, N_EDGE_DMAS * 16)
            for p, g in parts:
                nc.gpsimd.tensor_scalar(seg_f[p, g], dst_i[p, g], float(T), None, ALU.mult)
                nc.gpsimd.tensor_copy(rel_f[p, g], ety_i[p, g])
                last = nc.gpsimd.tensor_copy(src_f[p, g], src_i[p, g])
            last.then_inc(s_conv, 1)
            pool.wait_ge(s_conv, 1)
            for p, g in parts:
                last = nc.gpsimd.tensor_tensor(seg_f[p, g], seg_f[p, g], rel_f[p, g], ALU.add)
            last.then_inc(s_conv, 1)
            pool.wait_ge(s_conv, 2)
            if OVERLAP:
                nc.gpsimd.affine_select(out=seg_f[0:RL, G - 1, 0:OVERLAP], in_=seg_f[0:RL, G - 1, 0:OVERLAP],
                                        compare_op=ALU.is_gt, fill=-1.0, base=NT - 1 - (G - 1) * P,
                                        pattern=[[0, OVERLAP]], channel_multiplier=-1).then_inc(s_conv, 1)
            for c, (a, b) in enumerate(CH):
                pool.wait_ge(s_mid, c + 1)
                nc.gpsimd.tensor_tensor(h3[:, a:b, 2], rem[:, a:b], h3[:, a:b, 1], ALU.subtract).then_inc(s_lo, 1)
            nc.gpsimd.iota(iota_g[:], [[1, GW]], base=0, channel_multiplier=0,
                           allow_small_or_imprecise_dtypes=True)
            nc.gpsimd.memset(zeros[:], 0.0).then_inc(s_zero, 1)
            pool.wait_ge(s_table, 16 * N_TAB)
            pool.wait_ge(s_flag, 1)
            unordered = pool.value_load(flag[0:1, 0:1])

            def gather(slot, idx):
                return nc.gpsimd.indirect_dma_start(rows[:, slot].rearrange("p k d -> p (k d)"), None, table,
                                                    bass.IndirectOffsetOnAxis(ap=idx, axis=0))

            def step(s, n):
                t0 = s * STEP
                for u in range(n):
                    if u % STAGE == 0:
                        pool.wait_ge(s_staged, s * NSTAGE + u // STAGE + 1)
                    if u % FREED == 0 and not (isinstance(s, int) and s == 0 and u < SLOTS):
                        pool.wait_ge(s_tile, t0 + u - SLOTS + FREED)
                        pool.nop(nofuse=True)
                    gather(u % SLOTS, stage[:, u // STAGE, u % STAGE:u % STAGE + 1]).then_inc(s_row[u % SLOTS], 16)

            with pool.If(unordered < 1):
                step(0, STEP)
                with pool.Fori(1, LAST) as s:
                    step(s, STEP)
                step(LAST, tiles_of(LAST))
            with pool.Else():
                with pool.Fori(0, NB * GQ) as w:
                    with pool.Fori(0, NT) as t:
                        k = w * NT + t
                        pool.wait_ge(s_gstaged, k + 1)
                        pool.nop(nofuse=True)
                        gather(0, stage[:, 0, 0:1]).then_inc(s_growd, 16)

        @block.scalar
        def _(act):
            def mid(c):
                a, b = CH[c]
                act.wait_ge(s_rem, c + 1)
                nc.scalar.activation(h3[:, a:b, 1], rem[:, a:b], ACT.Copy).then_inc(s_mid, 1)

            act.dma_start(dst_i[:, 0:GF], dst[0:GF * P * P].rearrange("(g r e) -> r g e", r=P, e=P)).then_inc(s_edges, 16)
            act.dma_start(src_i[:, 0:GF], src[0:GF * P * P].rearrange("(g r e) -> r g e", r=P, e=P)).then_inc(s_edges, 16)
            act.dma_start(ety_i[:, 0:GF], etype[0:GF * P * P].rearrange("(g r e) -> r g e", r=P, e=P)).then_inc(s_edges, 16)
            for to, frm in ((dst_i, dst), (src_i, src), (ety_i, etype)):
                lo = GF * P * P
                if FULL_ROWS:
                    act.dma_start(to[0:FULL_ROWS, GF], frm[lo:lo + FULL_ROWS * P].rearrange("(r e) -> r e", e=P)).then_inc(s_edges, 16)
                if OVERLAP:
                    act.dma_start(to[RL - 1:RL, G - 1], frm[E - P:E].rearrange("(r e) -> r e", e=P)).then_inc(s_edges, 16)
            act.dma_start(nty[:, 0:NB - 1], ntype[0:(NB - 1) * P].rearrange("(b p) -> p b", p=P),
                          allow_slow_non_contiguous=True).then_inc(s_w, 16)
            act.wait_ge(s_xpad, 1)
            act.dma_start(nty[0:NROW, LAST:NB], ntype[LAST * P:N].rearrange("(p o) -> p o", o=1),
                          allow_slow_non_contiguous=True).then_inc(s_w, 16)
            act.dma_start(nty_row[:, 0:N], ntype.rearrange("(o n) -> o n", o=1).broadcast_to([NTY, N])).then_inc(s_w, 16)

            act.wait_ge(s_const, 1)

            def deviation(c):
                a, b = CH[c]
                act.wait_ge(s_var, c + 1)
                nc.scalar.activation(std[:, a:b], mv[:, a:b, 1], ACT.Sqrt, bias=eps[:, 0:1]).then_inc(s_std, 1)

            deviation(0)
            for c, (a, b) in enumerate(CH):
                if c + 1 < NCHUNK:
                    deviation(c + 1)
                act.wait_ge(s_y, c + 1)
                nc.scalar.activation(h3[:, a:b, 0], h[:, a:b], ACT.Relu).then_inc(s_hi, 1)
                act.wait_ge(s_hi, c + 1)
                nc.scalar.activation(h[:, a:b], h[:, a:b], ACT.Relu).then_inc(s_h, 1)
                if c:
                    mid(c - 1)
            mid(NCHUNK - 1)

            act.wait_ge(s_pT, 1)
            for k in range(-(-G // 4)):
                w = min(NT, 4 * (k + 1) * P) - 4 * k * P
                last = nc.scalar.activation(src_T[:, 4 * k * P:4 * k * P + w], p_tile[k][:, 0:w], ACT.Copy)
            last.then_inc(s_srcT, 1)

            def stage_copy(j, t):
                act.nop(nofuse=True)
                nc.scalar.activation(stage[:, j], src_T[:, ds(t, STAGE)], ACT.Copy).then_inc(s_staged, 1)

            act.wait_ge(s_srcT, 1)
            act.wait_ge(s_flag, 1)
            unordered = act.value_load(flag[0:1, 0:1])

            def prep(b, filled):
                filled()
                act.wait_ge(s_prod, b * 6 + 1)
                col = ring_col(b)
                act.nop(nofuse=True)
                nc.scalar.activation(sums[:], ring[:, 0, ds(col, BC)].rearrange("p (n t) -> p t n", t=T), ACT.Copy)
                nc.scalar.activation(cnt_row[0:1], ring[0:1, 1, ds(col, BC)].rearrange("p (n t) -> p t n", t=T), ACT.Copy)
                nc.scalar.activation(hT_b[:], hT[:, ds(b * P, P)], ACT.Copy).then_inc(s_prep, 1)
                if isinstance(b, int) and b == LAST:
                    return
                act.wait_ge(s_prep, b + 1)
                act.nop(nofuse=True)
                nc.scalar.activation(ring[:, 0, ds(col, BC)], zeros[:], ACT.Copy)
                nc.scalar.activation(ring[:, 1, ds(col, BC)], zeros[:], ACT.Copy).then_inc(s_zeroed, 1)

            def hT_and_ring():
                act.wait_ge(s_pT, 3)
                for k in range(-(-G // 4)):
                    w = min(NT, 4 * (k + 1) * P) - 4 * k * P
                    last = nc.scalar.activation(seg_T[:, 4 * k * P:4 * k * P + w], p_prod[k][:, 0:w], ACT.Copy)
                last.then_inc(s_segT, 1)
                for r in range(HT_ROUNDS):
                    act.wait_ge(s_htp, r + 1)
                    w = min(4, NB - 4 * r) * P
                    nc.scalar.activation(hT[:, 4 * r * P:4 * r * P + w], p_prod[r % 2][:, 0:w], ACT.Copy).then_inc(s_htc, 1)
                act.wait_ge(s_zero, 1)
                act.wait_ge(s_lo, NCHUNK)
                for a in range(2):
                    for c in range(late, RC, BC):
                        nc.scalar.activation(ring[:, a, c:c + BC], zeros[:], ACT.Copy)
                    last = nc.scalar.activation(ring[:, a, RC:], zeros[:, 0:WIN], ACT.Copy)
                last.then_inc(s_ring1, 1)
                act.wait_ge(s_ring1, 1)
                act.wait_ge(s_htc, HT_ROUNDS)

            def step(s, n_next):
                for j in range(NSTAGE):
                    if j < n_next:
                        act.wait_ge(s_tile, s * STEP + (j + 1) * STAGE)
                        stage_copy(j, (s + 1) * STEP + j * STAGE)
                    if j == 0 and not (isinstance(s, int) and s == 0):
                        prep(s - 1, lambda: act.wait_ge(s_acc, block_in_ring(s)))

            with act.If(unordered < 1):
                for j in range(NSTAGE):
                    stage_copy(j, j * STAGE)
                hT_and_ring()
                step(0, NSTAGE)
                with act.Fori(1, LAST - 1) as s:
                    step(s, NSTAGE)
                step(LAST - 1, -(-tiles_of(LAST) // STAGE))
                step(LAST, 0)
                prep(LAST, lambda: act.wait_ge(s_acc, NT + 2 * LAST))
            with act.Else():
                hT_and_ring()
                with act.Fori(0, NB) as b:
                    with act.Fori(0, GQ) as q:
                        w = b * GQ + q
                        with act.Fori(0, NT) as t:
                            act.wait_ge(s_gmm, w * (NT + 2) + t + 1)
                            act.nop(nofuse=True)
                            nc.scalar.activation(stage[:, 0, 0:1], src_T[:, ds(t, 1)], ACT.Copy).then_inc(s_gstaged, 1)
                    prep(b, lambda: act.wait_ge(s_gcopied, (b + 1) * GQ + 1))

        @block.vector
        def _(dve):
            links = [0]

            def link(ins):
                links[0] += 1
                ins.then_inc(s_chain, 1)
                dve.wait_ge(s_chain, links[0])

            nc.vector.memset(nty[:, LAST:NB], 0)
            if NT < G * P:
                nc.vector.memset(src_T[:, NT:G * P], 0)
            nc.vector.memset(nty_row[:, N:NB * P], 0)
            nc.vector.memset(x_sb[:, LAST], 0.0).then_inc(s_xpad, 1)

            def normalise(c):
                a, b = CH[c]
                dve.wait_ge(s_std, c + 1)
                link(nc.vector.reciprocal(rstd[:, a:b], std[:, a:b]))
                link(nc.vector.scalar_tensor_tensor(nbias[:, a:b], mv[:, a:b, 0], -1.0, rstd[:, a:b],
                                                    ALU.mult, ALU.mult))
                for i in range(a, b):
                    last = nc.vector.tensor_scalar(h[:, i], x_sb[:, i], rstd[:, i:i + 1], nbias[:, i:i + 1],
                                                   ALU.mult, ALU.add)
                last.then_inc(s_y, 1)

            def remainder(c):
                a, b = CH[c]
                dve.wait_ge(s_h, c + 1)
                nc.vector.tensor_tensor(rem[:, a:b], h[:, a:b], h3[:, a:b, 0], ALU.subtract).then_inc(s_rem, 1)

            def edges():
                dve.wait_ge(s_edges, 16 * N_EDGE_DMAS)
                nc.vector.memset(bad[:], 0.0)
                for p, g in parts:
                    nc.vector.tensor_reduce(mn[p, g], dst_i[p, g], AX.X, ALU.min)
                    last = nc.vector.tensor_reduce(mx[p, g], dst_i[p, g], AX.X, ALU.max)
                link(last)
                dve.wait_ge(s_const, N_CONST)
                for p, g in parts:
                    nc.vector.tensor_scalar(mn16[p, g], mn[p, g], float(T), None, ALU.mult)
                    nc.vector.tensor_copy(off_i[p, g], mn[p, g])
                    last = nc.vector.tensor_tensor(dev[p, g], mn[p, g], pace[p, g], ALU.subtract)
                link(last)
                for p, g in parts:
                    nc.vector.tensor_tensor(bad[p, 0, g], mx[p, g], mn[p, g], ALU.subtract)
                    nc.vector.tensor_scalar(bad[p, 1, g], dev[p, g], float(-SLACK * PACE), None, ALU.is_lt)
                    nc.vector.tensor_scalar(bad[p, 2, g], dev[p, g], float(SLACK * PACE - WIN_NODES), None, ALU.is_gt)
                    last = nc.vector.tensor_scalar(off_i[p, g], off_i[p, g], RING_BLOCKS * P - 1, T.bit_length() - 1,
                                                   ALU.bitwise_and, ALU.logical_shift_left)
                link(last)
                for p, g in parts:
                    nc.vector.tensor_scalar(bad[p, 0, g], bad[p, 0, g], float(WIN_NODES - 1), None, ALU.is_gt)
                    last = nc.vector.tensor_copy(off_f[p, g], off_i[p, g])
                link(last)
                nc.vector.tensor_reduce(badsum[:], bad[:].rearrange("p a g -> p (a g)"), AX.X, ALU.add).then_inc(s_off, 1)
                dve.wait_ge(s_conv, N_CONV)
                for g in range(G):
                    r = P if g < GF else GR
                    last = nc.vector.tensor_scalar(rel_f[0:r, g], seg_f[0:r, g], mn16[0:r, g:g + 1], None, ALU.subtract)
                last.then_inc(s_relf, 1)

            for c, (a, b) in enumerate(CH):
                dve.wait_ge(s_xin[c], 16 * (2 if b == NB else 1))
                for i in range(a, b):
                    last = nc.vector.bn_stats(stats[:, i], x_sb[:, i])
                link(last)
                for i in range(a, b):
                    last = nc.vector.bn_aggr(mv[:, i], stats[:, i])
                last.then_inc(s_var, 1)
                if c:
                    normalise(c - 1)
                if c >= 2:
                    remainder(c - 2)
            normalise(NCHUNK - 1)
            remainder(NCHUNK - 2)
            edges()
            remainder(NCHUNK - 1)

            dve.wait_ge(s_pT, 4)
            for k in range(-(-G // 4)):
                w = (min(NT, 4 * (k + 1) * P) - 4 * k * P)
                nc.vector.tensor_copy(off_row[:, 4 * k * P:4 * k * P + w], (p_misc, p_aux)[k][0:1, 0:w])
            dve.wait_ge(s_pT, 5)
            nc.vector.tensor_copy(flag[:], p_tile[3][0:1, 511:512]).then_inc(s_flag, 1)
            dve.wait_ge(s_flag, 1)
            dve.wait_ge(s_relf, 1)
            for k in range(-(-G // 4)):
                w = min(NT, 4 * (k + 1) * P) - 4 * k * P
                last = nc.vector.tensor_copy(rel_T[:, 4 * k * P:4 * k * P + w], p_tile[2 + k][:, 0:w])
            link(last)
            dve.wait_ge(s_w, 16 * N_W)
            for t in range(NTY):
                nc.vector.tensor_scalar(nmask[:, t], nty[:], float(t), None, ALU.is_equal)
            dve.wait_ge(s_segT, 1)
            nc.vector.memset(win_neg[:], 0.0).then_inc(s_gcopied, 1)
            dve.wait_ge(s_gcopied, 1)
            dve.wait_ge(s_zero, 1)
            dve.wait_ge(s_ring0, 1)
            dve.wait_ge(s_ring1, 1)
            dve.sem_inc(s_used, 2)
            unordered = dve.value_load(flag[0:1, 0:1])

            def make_onehot(t, u, first):
                if not first:
                    dve.wait_ge(s_tile, t - ONEHOTS + 1)
                nc.vector.tensor_scalar(onehot[:, u % ONEHOTS], iota_w[:], rel_T[:, ds(t, 1)], None,
                                        ALU.is_equal).then_inc(s_onehot, 1)

            N_SUM = 1 + T + NTY

            def block_pieces(b):
                k = [0]

                def add(ins, reads_own=True):
                    if k[0] >= 2:
                        dve.wait_ge(s_dve, b * N_SUM + k[0] - 1)
                    ins(acc[:, k[0] % 2]).then_inc(s_dve, 1)
                    k[0] += 1

                def counts():
                    dve.wait_ge(s_cnt, b + 1)
                    nc.vector.tensor_scalar(cnt1[:], p_cnt, 1.0, None, ALU.max).then_inc(s_rc, 1)
                    nc.vector.tensor_scalar(has[:], p_cnt, 1.0, None, ALU.min).then_inc(s_has, 1)
                    dve.wait_ge(s_rc, 2 * b + 1)
                    nc.vector.reciprocal(rcnt[:], cnt1[:]).then_inc(s_rc, 1)

                def flags():
                    dve.wait_ge(s_hasT, b + 1)
                    nc.vector.tensor_copy(has_T[:], p_hasT)
                    nc.vector.tensor_scalar(nty_T[:], nty_row[:, ds(b * P, P)], part[0:NTY, 0:1], None,
                                            ALU.is_equal).then_inc(s_hasTc, 1)

                def group(g):
                    dve.wait_ge(s_prod, b * 6 + g + 2)
                    if g == 0:
                        add(lambda to: nc.vector.tensor_copy(to, p_bias))
                        dve.wait_ge(s_rc, 2 * b + 2)
                    for j in range(4):
                        w = (rcnt[:, 4 * g + j:4 * g + j + 1] if g < 4 else
                             nmask[:, 4 * (g - 4) + j, ds(b, 1)])
                        prod = p_prod[g % 2][:, j * D:(j + 1) * D]
                        if g == 0 and j == 0:
                            add(lambda to: nc.vector.tensor_scalar(to, prod, w, None, ALU.mult))
                        else:
                            add(lambda to: nc.vector.scalar_tensor_tensor(to, prod, w, to, ALU.mult, ALU.add))
                    dve.wait_ge(s_dve, b * N_SUM + k[0])
                    dve.sem_inc(s_used, 1)

                def last_group():
                    group(5)
                    assert k[0] == N_SUM
                    nc.vector.tensor_tensor(acc[:, 0], acc[:, 0], acc[:, 1], ALU.add).then_inc(s_sum, 1)
                    dve.wait_ge(s_stored, b + 1)
                    dve.wait_ge(s_sum, b + 1)
                    nc.vector.scalar_tensor_tensor(outb[:], acc[:, 0], 0.0, x_sb[:, ds(b, 1)].rearrange("p o d -> p (o d)"),
                                                   ALU.max, ALU.add).then_inc(s_final, 1)

                return {14: counts, 16: flags, 18: lambda: group(0), 21: lambda: group(1), 24: lambda: group(2),
                        26: lambda: group(3), 28: lambda: group(4), 30: last_group}

            off_reg = [dve.alloc_register(f"off{u}") for u in range(STAGE)]

            def step(s, n, pieces, fold):
                t0 = s * STEP
                left = dict(pieces)
                for u in range(n):
                    if u % STAGE == 0:
                        m = min(STAGE, n - u)
                        dve.reg_load(off_reg[0:m], off_row[0:1, ds(t0 + u, m)])
                        off = [dve.snap(r, min_val=0, max_val=RC - T) for r in off_reg[0:m]]
                    if not (isinstance(s, int) and t0 + u + AHEAD >= NT):
                        make_onehot(t0 + u + AHEAD, u + AHEAD, isinstance(s, int) and t0 + u + AHEAD < ONEHOTS)
                    dve.wait_ge(s_tile, t0 + u + 1)
                    if not (isinstance(s, int) and s == 0 and u == 0):
                        dve.wait_ge(s_acc, t0 + u + folds(s, u))
                    w = ring[:, :, ds(off[u % STAGE], WIN)]
                    nc.vector.tensor_tensor(w, w, p_tile[u % 4][:, 0:2 * WIN].rearrange("p (a c) -> p a c", a=2),
                                            ALU.add).then_inc(s_acc, 1)
                    if fold and u == SLACK - 1:
                        if not (isinstance(s, int) and s == 1):
                            dve.wait_ge(s_zeroed, s - 1)
                        done = block_in_ring(s) - 2
                        dve.wait_ge(s_acc, done)
                        nc.vector.tensor_tensor(ring[:, :, 0:WIN], ring[:, :, 0:WIN], ring[:, :, RC:RC + WIN],
                                                ALU.add).then_inc(s_acc, 1)
                        dve.wait_ge(s_acc, done + 1)
                        nc.vector.memset(ring[:, :, RC:RC + WIN], 0.0).then_inc(s_acc, 1)
                    if u in left:
                        left.pop(u)()
                for f in left.values():
                    f()

            with dve.If(unordered < 1):
                for t in range(AHEAD):
                    make_onehot(t, t, True)
                step(0, STEP, {}, False)
                with dve.Fori(1, LAST) as s:
                    step(s, STEP, block_pieces(s - 1), True)
                step(LAST, tiles_of(LAST), block_pieces(LAST - 1), True)
                for f in block_pieces(LAST).values():
                    f()
            with dve.Else():
                with dve.Fori(0, NB) as b:
                    with dve.Fori(0, GQ) as q:
                        w = b * GQ + q
                        with dve.Fori(0, NT) as t:
                            dve.wait_ge(s_gmm, w * (NT + 2) + t + 1)
                            nc.vector.tensor_scalar(onehot_g[:], iota_g[:], seg_T[:, ds(t, 1)], win_neg[:, 0:1],
                                                    ALU.subtract, ALU.is_equal).then_inc(s_goh, 1)
                        dve.wait_ge(s_gmm, (w + 1) * (NT + 2))
                        for a in range(2):
                            nc.vector.tensor_copy(ring[:, a, ds(ring_col(b) + q * GW, GW)], p_tile[a][:])
                        nc.vector.tensor_scalar(win_neg[:], win_neg[:], float(-GW), None, ALU.add).then_inc(s_gcopied, 1)
                        dve.wait_ge(s_gcopied, w + 2)
                    for f in block_pieces(b).values():
                        f()

        @block.tensor
        def _(pe):
            def turn(src3, banks):
                for g in range(G):
                    r = P if g < GF else GR
                    last = nc.tensor.transpose(banks[g // 4][:, (g % 4) * P:(g % 4) * P + r], src3[0:r, g], ident[0:r, 0:r])
                return last

            pe.wait_ge(s_const, N_CONST)
            pe.wait_ge(s_conv, 1)
            turn(src_f, p_tile[0:2]).then_inc(s_pT, 1)
            pe.wait_ge(s_conv, N_CONV)
            pe.wait_ge(s_relf, 1)
            turn(rel_f, p_tile[2:4]).then_inc(s_pT, 1)
            turn(seg_f, p_prod).then_inc(s_pT, 1)
            for g in range(G):
                r = P if g < GF else GR
                last = nc.tensor.matmul((p_misc, p_aux)[g // 4][0:1, (g % 4) * P:(g % 4) * P + r],
                                        lhsT=off_f[0:r, g:g + 1], rhs=ident[0:r, 0:r], start=True, stop=True)
            last.then_inc(s_pT, 1)
            nc.tensor.matmul(p_tile[3][0:1, 511:512], lhsT=badsum[:], rhs=one_f[:], start=True, stop=True).then_inc(s_pT, 1)
            pe.wait_ge(s_h, NCHUNK)
            pe.wait_ge(s_segT, 1)
            for r in range(HT_ROUNDS):
                if r >= 2:
                    pe.wait_ge(s_htc, r - 1)
                for i in range(4 * r, min(4 * r + 4, NB)):
                    last = nc.tensor.transpose(p_prod[r % 2][:, (i % 4) * P:(i % 4 + 1) * P], h[:, i], ident[:])
                last.then_inc(s_htp, 1)
            pe.wait_ge(s_htc, HT_ROUNDS)
            pe.wait_ge(s_srcT, 1)
            pe.wait_ge(s_w, 16 * N_W)
            pe.wait_ge(s_zero, 1)
            pe.sem_inc(s_prod, 1)
            pe.wait_ge(s_flag, 1)
            unordered = pe.value_load(flag[0:1, 0:1])

            def sums_of(bank_s, bank_c, slot, hot, start, last):
                for k in range(3):
                    nc.tensor.matmul(bank_s, lhsT=rows[:, slot, k], rhs=hot, start=start and k == 0, stop=last and k == 2)
                return nc.tensor.matmul(bank_c, lhsT=ones[:], rhs=hot, start=start, stop=last)

            def block_pieces(b):
                def counts():
                    pe.wait_ge(s_prep, b + 1)
                    pe.wait_ge(s_used, b * 6 + 2)
                    pe.nop(nofuse=True)
                    for t in range(T):
                        last = nc.tensor.transpose(p_cnt[:, t:t + 1], cnt_row[0:1, t], ident[0:1, 0:1])
                    last.then_inc(s_cnt, 1)

                def flags():
                    pe.wait_ge(s_has, b + 1)
                    nc.tensor.transpose(p_hasT, has[:], ident[:]).then_inc(s_hasT, 1)

                def bias():
                    pe.wait_ge(s_hasTc, b + 1)
                    nc.tensor.matmul(p_bias, lhsT=has_T[:], rhs=b_e[:], start=True, stop=False)
                    nc.tensor.matmul(p_bias, lhsT=nty_T[:], rhs=b_n[:], start=False, stop=True)

                def group(g):
                    pe.wait_ge(s_used, b * 6 + g + 1)
                    if g < 4:
                        for j in range(4):
                            last = nc.tensor.matmul(p_prod[g % 2][:, j * D:(j + 1) * D], lhsT=sums[:, 4 * g + j],
                                                    rhs=w_e[:, 4 * g + j], start=True, stop=True)
                    else:
                        j = 4 * (g - 4)
                        last = nc.tensor.matmul(p_prod[g % 2][:], lhsT=hT_b[:],
                                                rhs=w_n[:, j:j + 4].rearrange("p t f -> p (t f)"), start=True, stop=True)
                    last.then_inc(s_prod, 1)

                def first_group():
                    bias()
                    group(0)

                return {13: counts, 15: flags, 17: first_group, 20: lambda: group(1), 23: lambda: group(2),
                        25: lambda: group(3), 27: lambda: group(4), 29: lambda: group(5)}

            def step(s, n, pieces):
                t0 = s * STEP
                left = dict(pieces)
                for u in range(n):
                    pe.wait_ge(s_row[u % SLOTS], (s * (STEP // SLOTS) + u // SLOTS + 1) * 16)
                    pe.wait_ge(s_onehot, t0 + u + 1)
                    if not (isinstance(s, int) and s == 0 and u < 4):
                        pe.wait_ge(s_acc, t0 + u - 3 + (folds(s, u - 4) if u >= 4 else folds(s - 1, STEP)))
                    sums_of(p_tile[u % 4][:, 0:WIN], p_tile[u % 4][:, WIN:2 * WIN], u % SLOTS,
                            onehot[:, u % ONEHOTS], True, True).then_inc(s_tile, 1)
                    if u in left:
                        left.pop(u)()
                for f in left.values():
                    f()

            with pe.If(unordered < 1):
                step(0, STEP, {})
                with pe.Fori(1, LAST) as s:
                    step(s, STEP, block_pieces(s - 1))
                step(LAST, tiles_of(LAST), block_pieces(LAST - 1))
                for f in block_pieces(LAST).values():
                    f()
            with pe.Else():
                with pe.Fori(0, NB) as b:
                    with pe.Fori(0, GQ) as q:
                        w = b * GQ + q
                        pe.wait_ge(s_gcopied, w + 1)
                        nc.tensor.matmul(p_tile[0][:], lhsT=zeros[:, 0:P], rhs=zeros[:, 0:GW], start=True, stop=False)
                        nc.tensor.matmul(p_tile[1][:], lhsT=zeros[:, 0:P], rhs=zeros[:, 0:GW], start=True, stop=False).then_inc(s_gmm, 1)
                        with pe.Fori(0, NT) as t:
                            k = w * NT + t
                            pe.wait_ge(s_growd, (k + 1) * 16)
                            pe.wait_ge(s_goh, k + 1)
                            sums_of(p_tile[0][:], p_tile[1][:], 0, onehot_g[:], False, False).then_inc(s_gmm, 1)
                        nc.tensor.matmul(p_tile[0][:], lhsT=zeros[:, 0:P], rhs=zeros[:, 0:GW], start=False, stop=True)
                        nc.tensor.matmul(p_tile[1][:], lhsT=zeros[:, 0:P], rhs=zeros[:, 0:GW], start=False, stop=True).then_inc(s_gmm, 1)
                    for f in block_pieces(b).values():
                        f()


_INS = ["x", "src", "dst", "edge_type_16", "node_type_8", "L0_gnn_W_edge", "L0_gnn_b_edge", "L0_gnn_W_node", "L0_gnn_b_node"]


def kernel(**inputs):
    import numpy as np
    import concourse.bacc as bacc
    from concourse.bass_utils import run_bass_kernel_spmd

    nc = bacc.Bacc("TRN2", target_bir_lowering=False, num_devices=1)
    arrays, args = {}, []
    for name in _INS:
        a = np.ascontiguousarray(inputs[name])
        arrays[f"in_{name}"] = a
        args.append(nc.dram_tensor(f"in_{name}", a.shape, mybir.dt.from_np(a.dtype), kind="ExternalInput").ap())
    out = nc.dram_tensor("out_0", inputs["x"].shape, F32, kind="ExternalOutput").ap()
    gnn_program(nc, *args, out)
    r = run_bass_kernel_spmd(nc, [arrays], core_ids=[0])
    return r.results[0]["out_0"]
```

```python
from contextlib import ExitStack

import concourse.bass as bass
from concourse import mybir
from concourse.alu_op_type import AluOpType as ALU

ACT = mybir.ActivationFunctionType
AX = mybir.AxisListType
F32 = mybir.dt.float32
BF16 = mybir.dt.bfloat16
I32 = mybir.dt.int32

P = 128
EPS = 1e-5
STEP = 32
SLOTS = 16
FREED = 4
STAGE = 8
NSTAGE = STEP // STAGE
ONEHOTS = 16
BY_PE = (4, 10)
NPG = 5
BY_DVE = 3
PICKS = 8
PICK_GROUPS = 3
LAG = 3
AHEAD = 8
SLACK = 8
FOLD = 12
RING_BLOCKS = 4
WIN_NODES = 8
GEN_NODES = 32
ds = bass.ds


def gnn_program(nc, x, src, dst, etype, ntype, w_edge, b_edge, w_node, b_node, out):
    N, D = x.shape
    E = src.shape[0]
    T = w_edge.shape[0]
    NTY = w_node.shape[0]
    assert D == P and WIN_NODES * T == P and E >= P
    NB = -(-N // P)
    NT = -(-E // P)
    assert -(-NT // STEP) == NB and NB >= 5 and NT - (NB - 1) * STEP >= FOLD >= SLACK
    PACE = P // STEP
    G = -(-NT // P)
    GF, GR = NT // P, NT % P
    FULL_ROWS = E // P - GF * P
    RL = GR or P
    OVERLAP = NT * P - E
    NROW = N - (NB - 1) * P
    PICKS_AT_ONCE = -(-NB // (STEP // 2 - LAG))
    PICK_TILES = -(-NB // PICKS_AT_ONCE)
    FIRST_A = 1 + LAG
    FIRST_B = STEP // 2 + 1
    PICK_GROUP = -(-NB // NPG)
    NPD = BY_DVE * PICK_GROUP
    ACT_GROUPS = [(0, g) for g in range(BY_DVE, NPG)] + [(1, g) for g in range(NPG)]
    NPA = len(ACT_GROUPS)
    assert max(BY_PE) < FOLD and FIRST_A + PICK_TILES <= FIRST_B and FIRST_B + PICK_TILES <= STEP and NB > (NPG - 1) * PICK_GROUP
    BC = P * T
    RC = RING_BLOCKS * BC
    WIN = WIN_NODES * T
    GW = GEN_NODES * T
    GQ = BC // GW
    EDGES = [-(-NB * percent // 100) for percent in ((0, 28, 56, 80, 100) if NB >= 16 else (0, 50, 100))]
    NCHUNK = len(EDGES) - 1
    CH = [(EDGES[c], EDGES[c + 1]) for c in range(NCHUNK)]
    LAST = NB - 1

    table = nc.dram_tensor("h_table", (N, 3 * D), BF16, kind="Internal").ap()

    with ExitStack() as ctx:
        def sb(name, shape, dt):
            return ctx.enter_context(nc.sbuf_tensor(name, shape, dt))

        def pb(name, shape, dt=F32):
            return ctx.enter_context(nc.psum_tensor(name, shape, dt))

        def sem(name):
            return ctx.enter_context(nc.semaphore(name))

        x_sb = sb("x_sb", [P, NB, D], F32)
        h3 = sb("h3", [P, NB, 3, D], BF16)
        hT = sb("hT", [P, NB * P], F32)
        ring = sb("ring", [P, 2, RC + WIN], F32)
        sums = sb("sums", [P, T, P], F32)
        cnt_row = sb("cnt_row", [P, T, P], F32)

        def scratch(space, start, dt, *shape):
            n = shape[0] * shape[1]
            v = space[:, start:start + n]
            v = v.bitcast(I32) if dt is I32 else v
            return v.rearrange("p (a b) -> p a b", b=shape[1])

        late = RC // 2
        late_s, late_c = ring[:, 0, late:], ring[:, 1, late:]
        sums_v = sums[:].rearrange("p t n -> p (t n)")
        cnt_v = cnt_row[:].rearrange("p t n -> p (t n)")
        GE = G * P
        assert NB * D + GE <= late + WIN and 2 * GE <= BC
        h = scratch(late_s, 0, F32, NB, D)
        rem = scratch(late_c, 0, F32, NB, D)
        seg_f = scratch(late_s, NB * D, F32, G, P)
        rel_f = scratch(late_c, NB * D, F32, G, P)
        src_i = scratch(sums_v, 0, I32, G, P)
        dst_i = scratch(sums_v, GE, I32, G, P)
        ety_i = scratch(cnt_v, 0, I32, G, P)
        src_f = scratch(cnt_v, GE, F32, G, P)

        src_T = sb("src_T", [P, G * P], I32)
        rel_T = sb("rel_T", [P, G * P], F32)
        seg_T = sb("seg_T", [P, G * P], F32)
        off_row = sb("off_row", [1, G * P], I32)
        stage = sb("stage", [P, NSTAGE, STAGE], I32)
        rows = sb("rows", [P, SLOTS, 3, D], BF16)
        onehot = sb("onehot", [P, ONEHOTS, WIN], BF16)
        onehot_g = sb("onehot_g", [P, GW], BF16)
        iota_w = sb("iota_w", [P, WIN], BF16)
        iota_g = sb("iota_g", [P, GW], F32)
        win_neg = sb("win_neg", [P, 1], F32)
        ones = sb("ones", [P, P], BF16)
        one_f = sb("one_f", [P, 1], F32)
        zeros = sb("zeros", [P, BC], BF16)
        ident = sb("ident", [P, P], F32)
        node_id = sb("node_id", [P, NB], F32)
        neg_id = sb("neg_id", [P, NB], F32)
        src_b = sb("src_b", [P, 2, P], I32)
        pick_src = sb("pick_src", [P, PICKS, P], BF16)
        distance = sb("distance", [P, PICK_GROUP, P], BF16)
        pick_b = sb("pick_b", [P, PICK_GROUPS, PICK_GROUP, P], BF16)
        rows_pe = sb("rows_pe", [P, 2, 3, D], BF16)
        eps = sb("eps", [P, 1], F32)
        pace = sb("pace", [P, G], F32)
        stats = sb("stats", [P, NB, 6], F32)
        mv = sb("mv", [P, NB, 2], F32)
        std = sb("std", [P, NB], F32)
        rstd = sb("rstd", [P, NB], F32)
        nbias = sb("nbias", [P, NB], F32)
        mn = sb("mn", [P, G], F32)
        mx = sb("mx", [P, G], F32)
        mn16 = sb("mn16", [P, G], F32)
        dev = sb("dev", [P, G], F32)
        bad = sb("bad", [P, 3, G], F32)
        badsum = sb("badsum", [P, 1], F32)
        flag = sb("flag", [1, 1], I32)
        off_i = sb("off_i", [P, G], I32)
        off_f = sb("off_f", [P, G], F32)
        w_e = sb("w_e", [P, T, D], F32)
        w_n = sb("w_n", [P, NTY, D], F32)
        b_e = sb("b_e", [T, D], F32)
        b_n = sb("b_n", [NTY, D], F32)
        nty_row = sb("nty_row", [P, NB * P], I32)
        hT_m = sb("hT_m", [P, NTY, P], F32)
        cnt1 = sb("cnt1", [P, T], F32)
        rcnt = sb("rcnt", [P, T], F32)
        has = sb("has", [P, T], F32)
        has_T = sb("has_T", [T, P], F32)
        nty_T = sb("nty_T", [NTY, P], F32)
        rcnt_rem = sb("rcnt_rem", [P, T], F32)
        rcnt3 = sb("rcnt3", [P, 3, T], BF16)
        rcnt3_T = sb("rcnt3_T", [3 * T, P], BF16)
        ident_b = sb("ident_b", [P, P], BF16)
        pick = sb("pick", [3 * T, T], BF16)
        outb = sb("outb", [P, D], F32)

        p_tile = [pb(f"p_tile{i}", [P, 512]) for i in range(4)]
        p_spread = pb("p_spread", [P, 512])
        p_gather = pb("p_gather", [P, 512])
        p_two = (p_spread, p_gather)
        p_rows = p_gather[:, 0:3 * D]
        p_misc = pb("p_misc", [P, 512])
        p_aux = pb("p_aux", [P, 512])
        p_cnt = p_misc[:, 0:T]
        p_hasT = p_misc[0:T, 128:128 + P]
        p_rcntT = p_misc[0:3 * T, 256:256 + P]
        p_out = p_aux[:, 0:D]

        s_xin = [sem(f"s_xin{c}") for c in range(NCHUNK)]
        s_xpad = sem("s_xpad")
        s_edges = sem("s_edges")
        s_w = sem("s_w")
        s_const = sem("s_const")
        s_var = sem("s_var")
        s_std = sem("s_std")
        s_norm = sem("s_norm")
        s_y_act = sem("s_y_act")
        s_hi = sem("s_hi")
        s_rem = sem("s_rem")
        s_mid = sem("s_mid")
        s_lo = sem("s_lo")
        s_y = sem("s_y")
        s_conv = sem("s_conv")
        s_ring0 = sem("s_ring0")
        s_ring1 = sem("s_ring1")
        s_table = sem("s_table")
        s_chain = sem("s_chain")
        s_relf = sem("s_relf")
        s_bad = sem("s_bad")
        s_srcf = sem("s_srcf")
        s_etyf = sem("s_etyf")
        s_pT = sem("s_pT")
        s_srcT = sem("s_srcT")
        s_segT = sem("s_segT")
        s_flag = sem("s_flag")
        s_htp = sem("s_htp")
        s_htc = sem("s_htc")
        s_zero = sem("s_zero")
        s_row = [sem(f"s_row{k}") for k in range(SLOTS)]
        s_staged = sem("s_staged")
        s_onehot = sem("s_onehot")
        s_tile = sem("s_tile")
        s_acc = sem("s_acc")
        s_srcb = sem("s_srcb")
        s_picked = sem("s_picked")
        s_picks_used = sem("s_picks_used")
        s_distance = sem("s_distance")
        s_picked_b = sem("s_picked_b")
        s_picks_b_used = sem("s_picks_b_used")
        s_gathered = sem("s_gathered")
        s_prep = sem("s_prep")
        s_zeroed = sem("s_zeroed")
        s_cnt = sem("s_cnt")
        s_rc = sem("s_rc")
        s_has = sem("s_has")
        s_hasT = sem("s_hasT")
        s_hasTc = sem("s_hasTc")
        s_masked = sem("s_masked")
        s_node = sem("s_node")
        s_spread = sem("s_spread")
        s_scaled = sem("s_scaled")
        s_prod = sem("s_prod")
        s_final = sem("s_final")
        s_out = sem("s_out")
        s_stored = sem("s_stored")
        s_gstaged = sem("s_gstaged")
        s_growd = sem("s_growd")
        s_goh = sem("s_goh")
        s_gmm = sem("s_gmm")
        s_gcopied = sem("s_gcopied")

        N_CONST = 10
        N_EDGE_DMAS = 3 * (1 + bool(FULL_ROWS) + bool(OVERLAP))
        N_CONV = 2 + bool(OVERLAP)
        BY_ACT = max(1, NB // NCHUNK // 3)
        parts = [(slice(0, P), slice(0, GF)), (slice(0, GR), slice(GF, G))][:1 + bool(GR)]
        N_W = 5
        N_TAB = NCHUNK + 1
        HT_ROUNDS = -(-NB // 4)

        def tiles_of(s):
            return min(STEP, NT - s * STEP)

        def folds(s, u):
            if u >= FOLD:
                return 2 * s
            return 0 if isinstance(s, int) and s == 0 else 2 * (s - 1)

        def block_in_ring(s):
            return s * STEP + SLACK + folds(s, SLACK)

        def out_bank(b):
            return p_gather[:, 0:D] if isinstance(b, int) and b == LAST else p_out

        def spread_bank(b, g):
            if not isinstance(b, int) or b < LAST - 1:
                return p_spread
            n = tiles_of(LAST)
            return (p_spread, p_tile[n % 4], p_tile[(n + 1) % 4], p_tile[(n + 2) % 4])[g]

        def ring_col(b):
            return (b & (RING_BLOCKS - 1)) * BC

        block = ctx.enter_context(nc.Block())

        @block.sync
        def _(sp):
            for c, (a, b) in enumerate(CH):
                full = min(b, NB - 1)
                sp.dma_start(x_sb[:, a:full, :], x[a * P:full * P].rearrange("(b p) d -> p b d", p=P)).then_inc(s_xin[c], 16)
                if b == NB:
                    sp.wait_ge(s_xpad, 1)
                    sp.dma_start(x_sb[0:NROW, LAST, :], x[LAST * P:N]).then_inc(s_xin[c], 16)
            for to, frm in ((dst_i, dst), (src_i, src), (ety_i, etype)):
                lo = GF * P * P
                sp.dma_start(to[:, 0:GF], frm[0:lo].rearrange("(g r e) -> r g e", r=P, e=P)).then_inc(s_edges, 16)
                if FULL_ROWS:
                    sp.dma_start(to[0:FULL_ROWS, GF], frm[lo:lo + FULL_ROWS * P].rearrange("(r e) -> r e", e=P)).then_inc(s_edges, 16)
                if OVERLAP:
                    sp.dma_start(to[RL - 1:RL, G - 1], frm[E - P:E].rearrange("(r e) -> r e", e=P)).then_inc(s_edges, 16)
            sp.dma_start(nty_row[:, 0:N], ntype.rearrange("(o n) -> o n", o=1).broadcast_to([P, N])).then_inc(s_w, 16)
            sp.dma_start(w_e[:], w_edge.rearrange("t d f -> d t f")).then_inc(s_w, 16)
            sp.dma_start(w_n[:], w_node.rearrange("t d f -> d t f")).then_inc(s_w, 16)
            sp.dma_start(b_e[:], b_edge).then_inc(s_w, 16)
            sp.dma_start(b_n[:], b_node).then_inc(s_w, 16)
            for c, (a, b) in enumerate(CH):
                sp.wait_ge(s_lo, c + 1)
                full = min(b, NB - 1)
                sp.dma_start(table[a * P:full * P].rearrange("(b p) w -> p b w", p=P),
                             h3[:, a:full].rearrange("p b k d -> p b (k d)")).then_inc(s_table, 16)
                if b == NB:
                    sp.dma_start(table[LAST * P:N], h3[0:NROW, LAST].rearrange("p k d -> p (k d)")).then_inc(s_table, 16)
            sp.sem_inc(s_stored, 1)

            def store(b, row, n):
                sp.wait_ge(s_final, b + 2)
                sp.dma_start(out[ds(row, n)], outb[0:n, :]).then_inc(s_out, 16)
                sp.wait_ge(s_out, (b + 1) * 16)
                sp.sem_inc(s_stored, 1)

            with sp.Fori(0, NB - 1) as b:
                store(b, b * P, P)
            store(LAST, LAST * P, NROW)

        @block.gpsimd
        def _(pool):
            nc.gpsimd.memset(eps[:], EPS).then_inc(s_const, 1)
            nc.gpsimd.memset(one_f[:], 1.0).then_inc(s_const, 1)
            nc.gpsimd.memset(ident[:], 1.0).then_inc(s_const, 1)
            pool.wait_ge(s_const, 3)
            nc.gpsimd.affine_select(out=ident[:], in_=ident[:], compare_op=ALU.is_equal, fill=0.0, base=0,
                                    pattern=[[-1, P]], channel_multiplier=1).then_inc(s_const, 1)
            pool.wait_ge(s_const, 4)
            nc.gpsimd.tensor_copy(ident_b[:], ident[:]).then_inc(s_const, 1)
            nc.gpsimd.iota(pace[:], [[PACE * P, G]], base=0, channel_multiplier=PACE,
                           allow_small_or_imprecise_dtypes=True).then_inc(s_const, 1)
            nc.gpsimd.iota(neg_id[:], [[-P, NB]], base=0, channel_multiplier=-1,
                           allow_small_or_imprecise_dtypes=True).then_inc(s_const, 1)
            nc.gpsimd.iota(node_id[:], [[P, NB]], base=0, channel_multiplier=1,
                           allow_small_or_imprecise_dtypes=True).then_inc(s_const, 1)
            nc.gpsimd.memset(ones[:], 1.0).then_inc(s_const, 1)
            nc.gpsimd.iota(iota_w[:], [[1, WIN]], base=0, channel_multiplier=0,
                           allow_small_or_imprecise_dtypes=True).then_inc(s_const, 1)
            nc.gpsimd.iota(iota_g[:], [[1, GW]], base=0, channel_multiplier=0,
                           allow_small_or_imprecise_dtypes=True)
            nc.gpsimd.memset(zeros[:], 0.0).then_inc(s_zero, 1)
            nc.gpsimd.memset(ring[:, :, 0:BC], 0.0).then_inc(s_ring0, 1)
            pool.wait_ge(s_edges, N_EDGE_DMAS * 16)
            for p, g in parts:
                last = nc.gpsimd.tensor_scalar(seg_f[p, g], dst_i[p, g], float(T), None, ALU.mult)
            last.then_inc(s_conv, 1)

            def low_part(c):
                a, b = CH[c]
                pool.wait_ge(s_mid, c + 1)
                nc.gpsimd.tensor_tensor(h3[:, a:b, 2], rem[:, a:b], h3[:, a:b, 1], ALU.subtract).then_inc(s_lo, 1)

            for c in range(NCHUNK):
                low_part(c)
            pool.wait_ge(s_conv, 1)
            pool.wait_ge(s_etyf, 1)
            for p, g in parts:
                last = nc.gpsimd.tensor_tensor(seg_f[p, g], seg_f[p, g], rel_f[p, g], ALU.add)
            last.then_inc(s_conv, 1)
            pool.wait_ge(s_conv, 2)
            if OVERLAP:
                nc.gpsimd.affine_select(out=seg_f[0:RL, G - 1, 0:OVERLAP], in_=seg_f[0:RL, G - 1, 0:OVERLAP],
                                        compare_op=ALU.is_gt, fill=-1.0, base=NT - 1 - (G - 1) * P,
                                        pattern=[[0, OVERLAP]], channel_multiplier=-1).then_inc(s_conv, 1)
            pool.wait_ge(s_table, 16 * N_TAB)
            pool.wait_ge(s_flag, 1)
            unordered = pool.value_load(flag[0:1, 0:1])

            def gather(slot, idx):
                return nc.gpsimd.indirect_dma_start(rows[:, slot].rearrange("p k d -> p (k d)"), None, table,
                                                    bass.IndirectOffsetOnAxis(ap=idx, axis=0))

            def step(s, n):
                t0 = s * STEP
                for u in range(n):
                    if u % STAGE == 0:
                        pool.wait_ge(s_staged, s * NSTAGE + u // STAGE + 1)
                    if u % FREED == 0 and not (isinstance(s, int) and s == 0 and u < SLOTS):
                        pool.wait_ge(s_tile, t0 + u - SLOTS + FREED)
                        pool.nop(nofuse=True)
                    if u in BY_PE and not (isinstance(s, int) and s == 0):
                        continue
                    gather(u % SLOTS, stage[:, u // STAGE, u % STAGE:u % STAGE + 1]).then_inc(s_row[u % SLOTS], 16)

            with pool.If(unordered < 1):
                step(0, STEP)
                with pool.Fori(1, LAST) as s:
                    step(s, STEP)
                step(LAST, tiles_of(LAST))
            with pool.Else():
                with pool.Fori(0, NB * GQ) as w:
                    with pool.Fori(0, NT) as t:
                        k = w * NT + t
                        pool.wait_ge(s_gstaged, k + 1)
                        pool.nop(nofuse=True)
                        gather(0, stage[:, 0, 0:1]).then_inc(s_growd, 16)

        @block.scalar
        def _(act):
            def mid(c):
                a, b = CH[c]
                act.wait_ge(s_rem, c + 1)
                nc.scalar.activation(h3[:, a:b, 1], rem[:, a:b], ACT.Copy).then_inc(s_mid, 1)

            def load_sources(s):
                for k in range(2):
                    act.dma_start(src_b[:, k], src[ds((s * STEP + BY_PE[k]) * P, P)].rearrange("(o e) -> o e", o=1)
                                  .broadcast_to([P, P])).then_inc(s_srcb, 16)

            load_sources(1)
            act.wait_ge(s_const, 1)
            nc.scalar.activation(win_neg[:], eps[:], ACT.Sqrt).then_inc(s_std, 1)

            def deviation(c):
                a, b = CH[c]
                act.wait_ge(s_var, c + 1)
                nc.scalar.activation(std[:, a:b], mv[:, a:b, 1], ACT.Sqrt, bias=eps[:, 0:1]).then_inc(s_std, 1)

            deviation(0)
            for c, (a, b) in enumerate(CH):
                act.wait_ge(s_norm, c + 1)
                for i in range(a, a + BY_ACT):
                    last = nc.scalar.activation(h[:, i], x_sb[:, i], ACT.Identity, bias=nbias[:, i:i + 1],
                                                scale=rstd[:, i:i + 1])
                last.then_inc(s_y_act, 1)
                if c + 1 < NCHUNK:
                    deviation(c + 1)
                act.wait_ge(s_y, c + 1)
                act.wait_ge(s_y_act, c + 1)
                nc.scalar.activation(h3[:, a:b, 0], h[:, a:b], ACT.Relu).then_inc(s_hi, 1)
                if c:
                    mid(c - 1)
                if c == NCHUNK - 1:
                    act.wait_ge(s_edges, 16 * N_EDGE_DMAS)
                    for p, g in parts:
                        last = nc.scalar.activation(src_f[p, g], src_i[p, g], ACT.Copy)
                    last.then_inc(s_srcf, 1)
            mid(NCHUNK - 1)
            for p, g in parts:
                last = nc.scalar.activation(rel_f[p, g], ety_i[p, g], ACT.Copy)
            last.then_inc(s_etyf, 1)

            act.wait_ge(s_pT, 1)
            for k in range(-(-G // 4)):
                w = min(NT, 4 * (k + 1) * P) - 4 * k * P
                last = nc.scalar.activation(src_T[:, 4 * k * P:4 * k * P + w], p_tile[k][:, 0:w], ACT.Copy)
            last.then_inc(s_srcT, 1)

            def stage_copy(j, t):
                act.nop(nofuse=True)
                nc.scalar.activation(stage[:, j], src_T[:, ds(t, STAGE)], ACT.Copy).then_inc(s_staged, 1)

            act.wait_ge(s_srcT, 1)
            act.wait_ge(s_flag, 1)
            unordered = act.value_load(flag[0:1, 0:1])

            def prep(b):
                act.wait_ge(s_cnt, b + 1)
                act.nop(nofuse=True)
                nc.scalar.activation(cnt_row[0:1], ring[0:1, 1, ds(ring_col(b), BC)].rearrange("p (n t) -> p t n", t=T),
                                     ACT.Copy).then_inc(s_prep, 1)

            def clear(b):
                act.wait_ge(s_scaled, 4 * b + 5)
                act.nop(nofuse=True)
                col = ring_col(b)
                nc.scalar.activation(ring[:, 0, ds(col, BC)], zeros[:], ACT.Copy)
                nc.scalar.activation(ring[:, 1, ds(col, BC)], zeros[:], ACT.Copy).then_inc(s_zeroed, 1)

            def hT_and_ring():
                act.wait_ge(s_pT, 5)
                for k in range(-(-G // 4)):
                    w = min(NT, 4 * (k + 1) * P) - 4 * k * P
                    last = nc.scalar.activation(seg_T[:, 4 * k * P:4 * k * P + w], p_two[k][:, 0:w], ACT.Copy)
                last.then_inc(s_segT, 1)
                for r in range(HT_ROUNDS):
                    act.wait_ge(s_htp, r + 1)
                    w = min(4, NB - 4 * r) * P
                    nc.scalar.activation(hT[:, 4 * r * P:4 * r * P + w], p_two[r % 2][:, 0:w], ACT.Relu).then_inc(s_htc, 1)
                act.wait_ge(s_lo, NCHUNK)
                for a in range(2):
                    for c in range(late, RC, BC):
                        nc.scalar.activation(ring[:, a, c:c + BC], zeros[:], ACT.Copy)
                    last = nc.scalar.activation(ring[:, a, RC:], zeros[:, 0:WIN], ACT.Copy)
                last.then_inc(s_ring1, 1)
                act.sem_inc(s_zeroed, 2)

            def pick_sources(s, i):
                k, g = ACT_GROUPS[i]
                n = min(PICK_GROUP, NB - g * PICK_GROUP)
                if i == 0:
                    act.wait_ge(s_srcb, (s + 1) * 32)
                if i >= PICK_GROUPS:
                    k0, g0 = ACT_GROUPS[i - PICK_GROUPS]
                    act.wait_ge((s_picks_used, s_picks_b_used)[k0], s * NB + min((g0 + 1) * PICK_GROUP, NB))
                elif not (isinstance(s, int) and s == 0):
                    act.wait_ge(s_picks_b_used, s * NB)
                act.nop(nofuse=True)
                if not (isinstance(s, int) and s == 0 and i == 0):
                    act.wait_ge(s_picked_b, s * NPA + i)
                    act.nop(nofuse=True)
                for m in range(n):
                    j = g * PICK_GROUP + m
                    last = nc.scalar.activation(distance[:, m], src_b[:, k], ACT.Abs, bias=neg_id[:, j:j + 1])
                last.then_inc(s_distance, 1)
                act.wait_ge(s_distance, s * NPA + i + 1)
                act.nop(nofuse=True)
                nc.scalar.activation(pick_b[:, i % PICK_GROUPS, 0:n], distance[:, 0:n], ACT.Relu, bias=one_f[:, 0:1],
                                     scale=-1.0).then_inc(s_picked_b, 1)

            def rows_out(s, k):
                act.wait_ge((s_picks_used, s_picks_b_used)[k], (s + 1) * NB)
                act.nop(nofuse=True)
                nc.scalar.activation(rows_pe[:, k], p_rows.rearrange("p (k d) -> p k d", k=3), ACT.Copy).then_inc(s_gathered, 1)

            def step(s):
                first, last = isinstance(s, int) and s == 0, isinstance(s, int) and s == LAST - 1
                n_next = -(-tiles_of(LAST) // STAGE) if last else NSTAGE

                def next_indices(j):
                    if j < n_next:
                        act.wait_ge(s_tile, s * STEP + (j + 1) * STAGE)
                        stage_copy(j, (s + 1) * STEP + j * STAGE)

                pick_sources(s, 0)
                next_indices(0)
                if not first:
                    act.wait_ge(s_acc, block_in_ring(s))
                    prep(s - 1)
                for i in range(1, PICK_GROUPS):
                    pick_sources(s, i)
                next_indices(1)
                rows_out(s, 0)
                for i in range(PICK_GROUPS, NPA):
                    pick_sources(s, i)
                next_indices(2)
                if not last:
                    act.wait_ge(s_picked, (s + 1) * NPD)
                    act.wait_ge(s_picked_b, (s + 1) * NPA)
                    load_sources(s + 2)
                next_indices(3)
                rows_out(s, 1)
                if not first:
                    clear(s - 1)

            with act.If(unordered < 1):
                for j in range(NSTAGE):
                    stage_copy(j, j * STAGE)
                hT_and_ring()
                step(0)
                with act.Fori(1, LAST - 1) as s:
                    step(s)
                step(LAST - 1)
            with act.Else():
                hT_and_ring()
                with act.Fori(0, NB) as b:
                    with act.Fori(0, GQ) as q:
                        w = b * GQ + q
                        with act.Fori(0, NT) as t:
                            act.wait_ge(s_gmm, w * (NT + 2) + t + 1)
                            act.nop(nofuse=True)
                            nc.scalar.activation(stage[:, 0, 0:1], src_T[:, ds(t, 1)], ACT.Copy).then_inc(s_gstaged, 1)
                    act.wait_ge(s_gcopied, (b + 1) * GQ + 1)
                    prep(b)
                    clear(b)

        @block.vector
        def _(dve):
            links = [0]

            def link(ins):
                links[0] += 1
                ins.then_inc(s_chain, 1)
                dve.wait_ge(s_chain, links[0])

            if NT < G * P:
                nc.vector.memset(src_T[:, NT:G * P], 0)
            nc.vector.memset(nty_row[:, N:NB * P], 0)
            nc.vector.memset(x_sb[:, LAST], 0.0).then_inc(s_xpad, 1)

            def normalise(c):
                a, b = CH[c]
                dve.wait_ge(s_std, c + 2)
                link(nc.vector.reciprocal(rstd[:, a:b], std[:, a:b]))
                link(nc.vector.scalar_tensor_tensor(nbias[:, a:b], mv[:, a:b, 0], -1.0, rstd[:, a:b],
                                                    ALU.mult, ALU.mult))
                dve.sem_inc(s_norm, 1)
                for i in range(a + BY_ACT, b):
                    last = nc.vector.tensor_scalar(h[:, i], x_sb[:, i], rstd[:, i:i + 1], nbias[:, i:i + 1],
                                                   ALU.mult, ALU.add)
                last.then_inc(s_y, 1)

            def remainder(c):
                a, b = CH[c]
                dve.wait_ge(s_hi, c + 1)
                nc.vector.scalar_tensor_tensor(rem[:, a:b], h[:, a:b], 0.0, h3[:, a:b, 0], ALU.max, ALU.subtract).then_inc(s_rem, 1)

            def first_nodes():
                dve.wait_ge(s_edges, 16 * N_EDGE_DMAS)
                nc.vector.memset(bad[:], 0.0)
                for p, g in parts:
                    nc.vector.tensor_reduce(mn[p, g], dst_i[p, g], AX.X, ALU.min)

            def places():
                for p, g in parts:
                    last = nc.vector.tensor_reduce(mx[p, g], dst_i[p, g], AX.X, ALU.max)
                link(last)
                dve.wait_ge(s_const, N_CONST)
                for p, g in parts:
                    nc.vector.tensor_scalar(mn16[p, g], mn[p, g], float(T), None, ALU.mult)
                    nc.vector.tensor_copy(off_i[p, g], mn[p, g])
                    last = nc.vector.tensor_tensor(dev[p, g], mn[p, g], pace[p, g], ALU.subtract)
                link(last)
                for p, g in parts:
                    nc.vector.tensor_tensor(bad[p, 0, g], mx[p, g], mn[p, g], ALU.subtract)
                    nc.vector.tensor_scalar(bad[p, 1, g], dev[p, g], float(-SLACK * PACE), None, ALU.is_lt)
                    nc.vector.tensor_scalar(bad[p, 2, g], dev[p, g], float(SLACK * PACE - WIN_NODES), None, ALU.is_gt)
                    last = nc.vector.tensor_scalar(off_i[p, g], off_i[p, g], RING_BLOCKS * P - 1, T.bit_length() - 1,
                                                   ALU.bitwise_and, ALU.logical_shift_left)
                link(last)
                for p, g in parts:
                    nc.vector.tensor_scalar(bad[p, 0, g], bad[p, 0, g], float(WIN_NODES - 1), None, ALU.is_gt)
                    last = nc.vector.tensor_copy(off_f[p, g], off_i[p, g])
                link(last)
                nc.vector.tensor_reduce(badsum[:], bad[:].rearrange("p a g -> p (a g)"), AX.X, ALU.add).then_inc(s_bad, 1)

            def segments_in_windows():
                dve.wait_ge(s_conv, N_CONV)
                for g in range(G):
                    r = P if g < GF else GR
                    last = nc.vector.tensor_scalar(rel_f[0:r, g], seg_f[0:r, g], mn16[0:r, g:g + 1], None, ALU.subtract)
                last.then_inc(s_relf, 1)

            for c, (a, b) in enumerate(CH):
                dve.wait_ge(s_xin[c], 16 * (2 if b == NB else 1))
                for i in range(a, b):
                    last = nc.vector.bn_stats(stats[:, i], x_sb[:, i])
                link(last)
                for i in range(a, b):
                    last = nc.vector.bn_aggr(mv[:, i], stats[:, i])
                last.then_inc(s_var, 1)
                if c:
                    normalise(c - 1)
                if c >= 2:
                    remainder(c - 2)
            normalise(NCHUNK - 1)
            remainder(NCHUNK - 2)
            first_nodes()
            remainder(NCHUNK - 1)
            places()

            dve.wait_ge(s_pT, 2)
            nc.vector.tensor_copy(flag[:], p_tile[3][0:1, 511:512]).then_inc(s_flag, 1)
            segments_in_windows()
            dve.wait_ge(s_pT, 3)
            for k in range(-(-G // 4)):
                w = (min(NT, 4 * (k + 1) * P) - 4 * k * P)
                nc.vector.tensor_copy(off_row[:, 4 * k * P:4 * k * P + w], (p_misc, p_aux)[k][0:1, 0:w])
            dve.wait_ge(s_pT, 4)
            for k in range(-(-G // 4)):
                w = min(NT, 4 * (k + 1) * P) - 4 * k * P
                last = nc.vector.tensor_copy(rel_T[:, 4 * k * P:4 * k * P + w], p_tile[2 + k][:, 0:w])
            link(last)
            link(nc.vector.tensor_reduce(rcnt_rem[0:3 * T], ident[0:3 * T, 0:3 * T].rearrange("p (k t) -> p t k", t=T),
                                         AX.X, ALU.add))
            nc.vector.tensor_copy(pick[:], rcnt_rem[0:3 * T])
            dve.wait_ge(s_w, 16 * N_W)
            dve.wait_ge(s_segT, 1)
            nc.vector.memset(win_neg[:], 0.0).then_inc(s_gcopied, 1)
            dve.wait_ge(s_gcopied, 1)
            nc.vector.memset(ring[:, :, BC:late], 0.0).then_inc(s_ring0, 1)
            dve.wait_ge(s_ring0, 2)
            dve.wait_ge(s_flag, 1)
            dve.sem_inc(s_scaled, 1)
            dve.sem_inc(s_final, 1)
            unordered = dve.value_load(flag[0:1, 0:1])

            def make_onehot(t, u, first):
                if not first:
                    dve.wait_ge(s_tile, t - ONEHOTS + 1)
                nc.vector.tensor_scalar(onehot[:, u % ONEHOTS], iota_w[:], rel_T[:, ds(t, 1)], None,
                                        ALU.is_equal).then_inc(s_onehot, 1)

            def masked(b, k):
                if k == 0:
                    dve.wait_ge(s_node, b + 1)
                for t in (2 * k, 2 * k + 1):
                    last = nc.vector.scalar_tensor_tensor(hT_m[:, t], nty_row[:, ds(b * P, P)], float(t),
                                                          hT[:, ds(b * P, P)], ALU.is_equal, ALU.mult)
                last.then_inc(s_masked, 1)

            def counts(b):
                dve.wait_ge(s_cnt, b + 2)
                nc.vector.tensor_scalar(cnt1[:], p_cnt, 1.0, None, ALU.max).then_inc(s_rc, 1)
                nc.vector.tensor_scalar(has[:], p_cnt, 1.0, None, ALU.min).then_inc(s_has, 1)

            def inverse(b):
                dve.wait_ge(s_rc, 5 * b + 1)
                nc.vector.reciprocal(rcnt[:], cnt1[:]).then_inc(s_rc, 1)

            def first_part(b):
                dve.wait_ge(s_rc, 5 * b + 2)
                nc.vector.tensor_copy(rcnt3[:, 0], rcnt[:]).then_inc(s_rc, 1)

            def second_part(b):
                dve.wait_ge(s_rc, 5 * b + 3)
                nc.vector.tensor_tensor(rcnt_rem[:], rcnt[:], rcnt3[:, 0], ALU.subtract).then_inc(s_rc, 1)
                dve.wait_ge(s_rc, 5 * b + 4)
                nc.vector.tensor_copy(rcnt3[:, 1], rcnt_rem[:]).then_inc(s_rc, 1)

            def third_part(b):
                dve.wait_ge(s_rc, 5 * b + 5)
                nc.vector.tensor_tensor(rcnt3[:, 2], rcnt_rem[:], rcnt3[:, 1], ALU.subtract).then_inc(s_has, 1)

            def flags(b):
                dve.wait_ge(s_hasT, b + 1)
                nc.vector.tensor_copy(rcnt3_T[:], p_rcntT)
                nc.vector.tensor_copy(has_T[:], p_hasT)
                nc.vector.tensor_scalar(nty_T[:], nty_row[0:NTY, ds(b * P, P)], node_id[0:NTY, 0:1], None,
                                        ALU.is_equal).then_inc(s_hasTc, 1)

            def scale(b, g):
                dve.wait_ge(s_spread, 4 * b + g + 1)
                dve.wait_ge(s_prod, 4 * b + g + 1)
                own = ring[:, 0, ds(ring_col(b), BC)].rearrange("p (n t) -> p t n", t=T)
                nc.vector.tensor_tensor(sums[:, 4 * g:4 * g + 4], own[:, 4 * g:4 * g + 4],
                                        spread_bank(b, g)[:].rearrange("p (t n) -> p t n", n=P),
                                        ALU.mult).then_inc(s_scaled, 1)

            def final(b):
                dve.wait_ge(s_prod, 4 * b + 8)
                dve.wait_ge(s_stored, b + 1)
                nc.vector.scalar_tensor_tensor(outb[:], out_bank(b), 0.0, x_sb[:, ds(b, 1)].rearrange("p o d -> p (o d)"),
                                               ALU.max, ALU.add).then_inc(s_final, 1)

            def part_of_block(b, u):
                if u == 12:
                    counts(b)
                    inverse(b)
                if u == 13:
                    first_part(b)
                    second_part(b)
                    third_part(b)
                if u in (14, 15):
                    masked(b, u - 14)
                if u == 16:
                    flags(b)
                if u in (17, 18):
                    masked(b, u - 15)
                if u in (19, 22, 25, 28):
                    scale(b, (u - 19) // 3)
                if u == 31:
                    final(b)

            def part_of_last_two(u, n):
                if u in (0, 1):
                    masked(LAST - 1, 2 * u)
                    masked(LAST - 1, 2 * u + 1)
                if u in (4, 5, 6):
                    masked(LAST, u - 4)
                if u == 6:
                    masked(LAST, 3)
                if u == 8:
                    counts(LAST - 1)
                    inverse(LAST - 1)
                if u == 9:
                    first_part(LAST - 1)
                    second_part(LAST - 1)
                    third_part(LAST - 1)
                if u == 10:
                    flags(LAST - 1)
                if u == min(max(n - 2, 12), n - 1):
                    scale(LAST - 1, 0)
                if u == n - 1:
                    scale(LAST - 1, 1)
                    counts(LAST)
                    inverse(LAST)
                    first_part(LAST)
                    second_part(LAST)
                    third_part(LAST)
                    scale(LAST - 1, 2)
                    scale(LAST - 1, 3)
                    flags(LAST)
                    scale(LAST, 0)
                    scale(LAST, 1)
                    final(LAST - 1)
                    scale(LAST, 2)
                    scale(LAST, 3)
                    final(LAST)

            def pick_sources(s, u):
                first = (u + LAG - FIRST_A) * PICKS_AT_ONCE
                for j in range(max(first, 0), min(first + PICKS_AT_ONCE, NPD)):
                    if j == 0:
                        dve.wait_ge(s_srcb, (s + 1) * 32)
                    if not (isinstance(s, int) and s == 0 and j < PICKS):
                        dve.wait_ge(s_picks_used, s * NB + max(j - PICKS + 1, 0))
                    nc.vector.tensor_scalar(pick_src[:, j % PICKS], src_b[:, 0], node_id[:, j:j + 1], None, ALU.is_equal).then_inc(s_picked, 1)

            off_reg = [dve.alloc_register(f"off{u}") for u in range(STAGE)]

            def step(s, n):
                t0 = s * STEP
                for u in range(n):
                    if u % STAGE == 0:
                        m = min(STAGE, n - u)
                        dve.reg_load(off_reg[0:m], off_row[0:1, ds(t0 + u, m)])
                        off = [dve.snap(r, min_val=0, max_val=RC - T) for r in off_reg[0:m]]
                    if not (isinstance(s, int) and t0 + u + AHEAD >= NT):
                        make_onehot(t0 + u + AHEAD, u + AHEAD, isinstance(s, int) and t0 + u + AHEAD < ONEHOTS)
                    dve.wait_ge(s_tile, t0 + u + 1)
                    if not (isinstance(s, int) and s == 0 and u == 0):
                        dve.wait_ge(s_acc, t0 + u + folds(s, u))
                    w = ring[:, :, ds(off[u % STAGE], WIN)]
                    nc.vector.tensor_tensor(w, w, p_tile[u % 4][:, 0:2 * WIN].rearrange("p (a c) -> p a c", a=2),
                                            ALU.add).then_inc(s_acc, 1)
                    if u == FOLD - 1 and not (isinstance(s, int) and s == 0):
                        dve.wait_ge(s_zeroed, s + 1)
                        if not (isinstance(s, int) and s == LAST):
                            dve.wait_ge(s_prep, s)
                        elif (LAST - 1) % RING_BLOCKS == 0:
                            dve.wait_ge(s_cnt, LAST + 1)
                        done = t0 + FOLD + folds(s, u)
                        dve.wait_ge(s_acc, done)
                        nc.vector.tensor_tensor(ring[:, :, 0:WIN], ring[:, :, 0:WIN], ring[:, :, RC:RC + WIN],
                                                ALU.add).then_inc(s_acc, 1)
                        dve.wait_ge(s_acc, done + 1)
                        nc.vector.memset(ring[:, :, RC:RC + WIN], 0.0).then_inc(s_acc, 1)
                    if isinstance(s, int) and s == LAST:
                        part_of_last_two(u, n)
                    elif not isinstance(s, int):
                        part_of_block(s - 1, u)
                    if not (isinstance(s, int) and s == LAST):
                        pick_sources(s, u)

            with dve.If(unordered < 1):
                for t in range(AHEAD):
                    make_onehot(t, t, True)
                step(0, STEP)
                dve.wait_ge(s_ring1, 1)
                with dve.Fori(1, LAST) as s:
                    step(s, STEP)
                step(LAST, tiles_of(LAST))
            with dve.Else():
                dve.wait_ge(s_ring1, 1)
                dve.wait_ge(s_srcb, 32)
                with dve.Fori(0, NB) as b:
                    with dve.Fori(0, GQ) as q:
                        w = b * GQ + q
                        with dve.Fori(0, NT) as t:
                            dve.wait_ge(s_gmm, w * (NT + 2) + t + 1)
                            nc.vector.tensor_scalar(onehot_g[:], iota_g[:], seg_T[:, ds(t, 1)], win_neg[:, 0:1],
                                                    ALU.subtract, ALU.is_equal).then_inc(s_goh, 1)
                        dve.wait_ge(s_gmm, (w + 1) * (NT + 2))
                        for a in range(2):
                            nc.vector.tensor_copy(ring[:, a, ds(ring_col(b) + q * GW, GW)], p_tile[a][:])
                        nc.vector.tensor_scalar(win_neg[:], win_neg[:], float(-GW), None, ALU.add).then_inc(s_gcopied, 1)
                        dve.wait_ge(s_gcopied, w + 2)
                    for u in range(STEP):
                        part_of_block(b, u)

        @block.tensor
        def _(pe):
            def turn(src3, banks):
                for g in range(G):
                    r = P if g < GF else GR
                    last = nc.tensor.transpose(banks[g // 4][:, (g % 4) * P:(g % 4) * P + r], src3[0:r, g], ident[0:r, 0:r])
                return last

            pe.wait_ge(s_const, N_CONST)
            pe.wait_ge(s_srcf, 1)
            turn(src_f, p_tile[0:2]).then_inc(s_pT, 1)
            pe.wait_ge(s_bad, 1)
            nc.tensor.matmul(p_tile[3][0:1, 511:512], lhsT=badsum[:], rhs=one_f[:], start=True, stop=True).then_inc(s_pT, 1)
            for g in range(G):
                r = P if g < GF else GR
                last = nc.tensor.matmul((p_misc, p_aux)[g // 4][0:1, (g % 4) * P:(g % 4) * P + r],
                                        lhsT=off_f[0:r, g:g + 1], rhs=ident[0:r, 0:r], start=True, stop=True)
            last.then_inc(s_pT, 1)
            pe.wait_ge(s_flag, 1)
            pe.wait_ge(s_conv, N_CONV)
            pe.wait_ge(s_relf, 1)
            turn(rel_f, p_tile[2:4]).then_inc(s_pT, 1)
            turn(seg_f, p_two).then_inc(s_pT, 1)
            pe.wait_ge(s_y, NCHUNK)
            pe.wait_ge(s_y_act, NCHUNK)
            pe.wait_ge(s_segT, 1)
            for r in range(HT_ROUNDS):
                if r >= 2:
                    pe.wait_ge(s_htc, r - 1)
                for i in range(4 * r, min(4 * r + 4, NB)):
                    last = nc.tensor.transpose(p_two[r % 2][:, (i % 4) * P:(i % 4 + 1) * P], h[:, i], ident[:])
                last.then_inc(s_htp, 1)
            pe.wait_ge(s_htc, HT_ROUNDS)
            pe.wait_ge(s_srcT, 1)
            pe.wait_ge(s_w, 16 * N_W)
            pe.wait_ge(s_zero, 1)
            pe.sem_inc(s_prod, 4)
            pe.sem_inc(s_node, 1)
            pe.sem_inc(s_cnt, 1)
            pe.wait_ge(s_flag, 1)
            unordered = pe.value_load(flag[0:1, 0:1])

            def sums_of(bank_s, bank_c, of_h, hot, start, last):
                for k in range(3):
                    nc.tensor.matmul(bank_s, lhsT=of_h[:, k], rhs=hot, start=start and k == 0, stop=last and k == 2)
                return nc.tensor.matmul(bank_c, lhsT=ones[:], rhs=hot, start=start, stop=last)

            def node(b, k):
                pe.wait_ge(s_masked, 4 * b + k + 1)
                if k == 0:
                    if isinstance(b, int) and b == LAST:
                        pe.wait_ge(s_gathered, 2 * LAST)
                    else:
                        pe.wait_ge(s_final, b + 1)
                for t in (2 * k, 2 * k + 1):
                    last = nc.tensor.matmul(out_bank(b), lhsT=hT_m[:, t], rhs=w_n[:, t], start=t == 0, stop=False)
                if k == NTY // 2 - 1:
                    last.then_inc(s_node, 1)

            def counts(b):
                if not isinstance(b, int):
                    pe.wait_ge(s_prep, b + 1)
                else:
                    pe.wait_ge(s_acc, block_in_ring(LAST) if b < LAST else NT + 2 * LAST)
                pe.nop(nofuse=True)
                for t in range(T):
                    row = (cnt_row[0:1, t] if not isinstance(b, int) else
                           ring[0:1, 1, ring_col(b):ring_col(b) + BC].rearrange("p (n t) -> p t n", t=T)[:, t])
                    last = nc.tensor.transpose(p_cnt[:, t:t + 1], row, ident[0:1, 0:1])
                last.then_inc(s_cnt, 1)

            def flags(b):
                pe.wait_ge(s_has, 2 * b + 2)
                nc.tensor.matmul(p_rcntT, lhsT=rcnt3[:].rearrange("p k t -> p (k t)"), rhs=ident_b[:], start=True, stop=True)
                nc.tensor.transpose(p_hasT, has[:], ident[:]).then_inc(s_hasT, 1)

            def spread(b, g):
                if not isinstance(b, int):
                    pe.wait_ge(s_scaled, 4 * b + g + 1)
                elif b == LAST:
                    pe.wait_ge(s_scaled, 4 * b + g - 2)
                elif g == 0:
                    pe.wait_ge(s_scaled, 4 * b + 1)
                else:
                    u = tiles_of(LAST) - 5 + g
                    pe.wait_ge(s_acc, LAST * STEP + u + 1 + folds(LAST, u))
                for j in range(4):
                    t = 4 * g + j
                    last = nc.tensor.matmul(spread_bank(b, g)[:, j * P:(j + 1) * P],
                                            lhsT=pick[:, t:t + 1].broadcast_to([3 * T, P]), rhs=rcnt3_T[:],
                                            start=True, stop=True)
                last.then_inc(s_spread, 1)

            def spreads(b, groups):
                pe.wait_ge(s_hasTc, b + 1)
                for g in groups:
                    spread(b, g)

            def bias(b):
                nc.tensor.matmul(out_bank(b), lhsT=has_T[:], rhs=b_e[:], start=False, stop=False)
                nc.tensor.matmul(out_bank(b), lhsT=nty_T[:], rhs=b_n[:], start=False, stop=False)

            def product(b, g):
                pe.wait_ge(s_scaled, 4 * b + g + 2)
                if g < 3 and not isinstance(b, int):
                    spread(b, g + 1)
                for t in range(4 * g, 4 * g + 4):
                    last = nc.tensor.matmul(out_bank(b), lhsT=sums[:, t], rhs=w_e[:, t], start=False, stop=t == T - 1)
                last.then_inc(s_prod, 1)

            def part_of_block(b, u):
                if u == 12:
                    counts(b)
                if u == 13 + LAG:
                    flags(b)
                if u in (14 + LAG, 15 + LAG):
                    node(b, u - 14 - LAG)
                if u == 16 + LAG:
                    spreads(b, (0,))
                    bias(b)
                if u in (17 + LAG, 18 + LAG):
                    node(b, u - 15 - LAG)
                if u in (19 + LAG, 22 + LAG, 25 + LAG, 28 + LAG):
                    product(b, (u - 19 - LAG) // 3)

            def part_of_last_two(u, n):
                if u in (2, 3):
                    node(LAST - 1, 2 * u - 4)
                    node(LAST - 1, 2 * u - 3)
                if u in (6, 7):
                    node(LAST, 2 * u - 12)
                    node(LAST, 2 * u - 11)
                if u == 8:
                    counts(LAST - 1)
                if u == 10:
                    flags(LAST - 1)
                if u == max(n - 3, 11):
                    spreads(LAST - 1, (0, 1))
                if u == n - 1:
                    spreads(LAST - 1, (2, 3))
                    counts(LAST)
                    bias(LAST - 1)
                    product(LAST - 1, 0)
                    flags(LAST)
                    product(LAST - 1, 1)
                    product(LAST - 1, 2)
                    spreads(LAST, (0, 1, 2, 3))
                    product(LAST - 1, 3)
                    bias(LAST)
                    for g in range(4):
                        product(LAST, g)

            def gather_sources(s, u):
                for k, at in enumerate((FIRST_A, FIRST_B)):
                    first = (u - at) * PICKS_AT_ONCE
                    for j in range(max(first, 0), min(first + PICKS_AT_ONCE, NB)):
                        if j == 0 and not (isinstance(s, int) and s == 0 and k == 0):
                            pe.wait_ge(s_gathered, 2 * s + k)
                        if k == 0 and j < NPD:
                            pe.wait_ge(s_picked, s * NPD + j + 1)
                            pick = pick_src[:, j % PICKS]
                        else:
                            i = ACT_GROUPS.index((k, j // PICK_GROUP))
                            if j % PICK_GROUP == 0:
                                pe.wait_ge(s_picked_b, s * NPA + i + 1)
                            pick = pick_b[:, i % PICK_GROUPS, j % PICK_GROUP]
                        nc.tensor.matmul(p_rows, lhsT=pick, rhs=h3[:, j].rearrange("p k d -> p (k d)"),
                                         start=j == 0, stop=j == NB - 1).then_inc((s_picks_used, s_picks_b_used)[k], 1)

            def step(s, n):
                t0 = s * STEP
                for u in range(n):
                    by_pe = u in BY_PE and not (isinstance(s, int) and s == 0)
                    if by_pe:
                        pe.wait_ge(s_gathered, 2 * s - 1 + BY_PE.index(u))
                    elif u % SLOTS in BY_PE:
                        pe.wait_ge(s_row[u % SLOTS], (s + 1 + u // SLOTS) * 16)
                    else:
                        pe.wait_ge(s_row[u % SLOTS], (s * (STEP // SLOTS) + u // SLOTS + 1) * 16)
                    pe.wait_ge(s_onehot, t0 + u + 1)
                    if not (isinstance(s, int) and s == 0 and u < 4):
                        pe.wait_ge(s_acc, t0 + u - 3 + (folds(s, u - 4) if u >= 4 else folds(s - 1, STEP)))
                    sums_of(p_tile[u % 4][:, 0:WIN], p_tile[u % 4][:, WIN:2 * WIN],
                            rows_pe[:, BY_PE.index(u)] if by_pe else rows[:, u % SLOTS],
                            onehot[:, u % ONEHOTS], True, True).then_inc(s_tile, 1)
                    if isinstance(s, int) and s == LAST:
                        part_of_last_two(u, n)
                    elif not isinstance(s, int):
                        part_of_block(s - 1, u)
                    if not (isinstance(s, int) and s == LAST):
                        gather_sources(s, u)

            with pe.If(unordered < 1):
                step(0, STEP)
                with pe.Fori(1, LAST) as s:
                    step(s, STEP)
                step(LAST, tiles_of(LAST))
            with pe.Else():
                with pe.Fori(0, NB) as b:
                    with pe.Fori(0, GQ) as q:
                        w = b * GQ + q
                        pe.wait_ge(s_gcopied, w + 1)
                        nc.tensor.matmul(p_tile[0][:], lhsT=zeros[:, 0:P], rhs=zeros[:, 0:GW], start=True, stop=False)
                        nc.tensor.matmul(p_tile[1][:], lhsT=zeros[:, 0:P], rhs=zeros[:, 0:GW], start=True, stop=False).then_inc(s_gmm, 1)
                        with pe.Fori(0, NT) as t:
                            k = w * NT + t
                            pe.wait_ge(s_growd, (k + 1) * 16)
                            pe.wait_ge(s_goh, k + 1)
                            sums_of(p_tile[0][:], p_tile[1][:], rows[:, 0], onehot_g[:], False, False).then_inc(s_gmm, 1)
                        nc.tensor.matmul(p_tile[0][:], lhsT=zeros[:, 0:P], rhs=zeros[:, 0:GW], start=False, stop=True)
                        nc.tensor.matmul(p_tile[1][:], lhsT=zeros[:, 0:P], rhs=zeros[:, 0:GW], start=False, stop=True).then_inc(s_gmm, 1)
                    for u in range(STEP):
                        part_of_block(b, u)


_INS = ["x", "src", "dst", "edge_type_16", "node_type_8", "L0_gnn_W_edge", "L0_gnn_b_edge", "L0_gnn_W_node", "L0_gnn_b_node"]


def kernel(**inputs):
    import numpy as np
    import concourse.bacc as bacc
    from concourse.bass_utils import run_bass_kernel_spmd

    nc = bacc.Bacc("TRN2", target_bir_lowering=False, num_devices=1)
    arrays, args = {}, []
    for name in _INS:
        a = np.ascontiguousarray(inputs[name])
        arrays[f"in_{name}"] = a
        args.append(nc.dram_tensor(f"in_{name}", a.shape, mybir.dt.from_np(a.dtype), kind="ExternalInput").ap())
    out = nc.dram_tensor("out_0", inputs["x"].shape, F32, kind="ExternalOutput").ap()
    gnn_program(nc, *args, out)
    r = run_bass_kernel_spmd(nc, [arrays], core_ids=[0])
    return r.results[0]["out_0"]
```
